# Optimizing a Trainium2 kernel written in Bass

```python
import numpy as np
import jax
import jax.numpy as jnp

def _softmax(x, axis=-1):
    return jax.nn.softmax(x, axis=axis)

def _gelu(x):
    return jax.nn.gelu(x, approximate=True)

def _silu(x):
    return jax.nn.silu(x)

def _sigmoid(x):
    return jax.nn.sigmoid(x)

def _layernorm(x, axis=-1, eps=1e-05):
    m = jnp.mean(x, axis=axis, keepdims=True)
    v = jnp.var(x, axis=axis, keepdims=True)
    return (x - m) / jnp.sqrt(v + eps)

def _scatter_add(tgt, idx, src, axis=0):
    return tgt.at[idx].add(src)

def _segment_sum(src, seg, n):
    return jax.ops.segment_sum(src, seg, n)
kernel_name = 'mk_adj_ffn_d1_adj_r2_748388'

def setup_inputs(seed: int=0):
    np.random.seed(seed)
    _w = jnp.asarray

    def _rec_inputs():
        import jax
        import jax.numpy as jnp
        _gk = jax.random.key(seed)
        x = -0.0001538 + 1 * jax.random.normal(jax.random.fold_in(_gk, 1), (128, 128, 384), jnp.float32)
        _a = jax.random.bernoulli(jax.random.fold_in(_gk, 2), 0.03125, (128, 128, 128))
        _af = _a.astype(jnp.float32)
        adj = _af
        return (x, adj)
    x, adj = _rec_inputs()

    def _L0_gnn_setup():
        import jax, jax.numpy as jnp
        import numpy as np
        LN_EPS = 1e-12

        def _digcn_forward(hidden_state, adjacency_matrix, Wl, bl, Ws, bs, Wr, br, ln_w, ln_b):
            B, S, D = hidden_state.shape
            temper = jnp.asarray(D, jnp.float32) ** 0.5
            i = jnp.arange(S)
            upper = (i[None, :] > i[:, None]).astype(hidden_state.dtype)
            lower = (i[None, :] < i[:, None]).astype(hidden_state.dtype)

            def layer(h, params):
                wl, b_l, ws, b_s, wr, b_r, g, beta = params
                u = jnp.einsum('bid,bjd->bij', h, h) / temper
                a = jax.nn.softmax(u, axis=-1)
                delta = a * adjacency_matrix
                attn = delta / (jnp.sum(delta, axis=-1, keepdims=True) + 1e-10)
                hl = h @ wl.T + b_l
                hs = h @ ws.T + b_s
                hr = h @ wr.T + b_r
                diag_a = jnp.diagonal(attn, axis1=1, axis2=2)
                ctx = jnp.einsum('bij,bjd->bid', attn * upper, hl) + diag_a[..., None] * hs + jnp.einsum('bij,bjd->bid', attn * lower, hr)
                mean = ctx.mean(-1, keepdims=True)
                var = ctx.var(-1, keepdims=True)
                o = (ctx - mean) / jnp.sqrt(var + LN_EPS) * g + beta
                return (jax.nn.relu(o), None)
            out, _ = jax.lax.scan(layer, hidden_state, (Wl, bl, Ws, bs, Wr, br, ln_w, ln_b))
            return out
        key = jax.random.key(seed)
        ks = jax.random.split(key, 6)
        B, S, D, L = (8, 512, 384, 2)
        scale = (1.0 / D) ** 0.5
        hidden_state = jax.random.normal(ks[0], (B, S, D), jnp.float32)
        adjacency_matrix = (jax.random.uniform(ks[1], (B, S, S)) < 0.05).astype(jnp.float32)
        Wl = jax.random.normal(ks[2], (L, D, D), jnp.float32) * scale
        Ws = jax.random.normal(ks[3], (L, D, D), jnp.float32) * scale
        Wr = jax.random.normal(ks[4], (L, D, D), jnp.float32) * scale
        bl = jnp.zeros((L, D), jnp.float32)
        bs = jnp.zeros((L, D), jnp.float32)
        br = jnp.zeros((L, D), jnp.float32)
        ln_w = jnp.ones((L, D), jnp.float32)
        ln_b = jnp.zeros((L, D), jnp.float32)
        return dict(hidden_state=hidden_state, adjacency_matrix=adjacency_matrix, Wl=Wl, bl=bl, Ws=Ws, bs=bs, Wr=Wr, br=br, ln_w=ln_w, ln_b=ln_b)
    _L0_gnn_all = _L0_gnn_setup()
    _L0_gnn_in = {k: v for k, v in _L0_gnn_all.items() if k in ('Wl', 'bl', 'Ws', 'bs', 'Wr', 'br', 'ln_w', 'ln_b')}
    del _L0_gnn_all

    def _L0_ffn_setup():
        import jax, jax.numpy as jnp
        import numpy as np
        H = 384
        R = 64
        E = 8
        B, S = (8, 1024)
        key = jax.random.key(seed)
        ks = jax.random.split(key, 10)
        s_in = 1.0 / np.sqrt(H)
        s_r = 1.0 / np.sqrt(R)
        return {'x': jax.random.normal(ks[0], (B, S, H), dtype=jnp.float32), 'enc_w': jax.random.uniform(ks[1], (H, R), jnp.float32, -s_in, s_in), 'enc_b': jax.random.uniform(ks[2], (R,), jnp.float32, -s_in, s_in), 'sw_w': jax.random.uniform(ks[3], (R, E), jnp.float32, -s_r, s_r), 'sw_b': jax.random.uniform(ks[4], (E,), jnp.float32, -s_r, s_r), 'w1': jax.random.uniform(ks[5], (E, H, R), jnp.float32, -s_in, s_in), 'b1': jax.random.uniform(ks[6], (E, R), jnp.float32, -s_in, s_in), 'w2': jax.random.uniform(ks[7], (E, R, H), jnp.float32, -s_r, s_r), 'b2': jax.random.uniform(ks[8], (E, H), jnp.float32, -s_r, s_r)}
    _L0_ffn_all = _L0_ffn_setup()
    _L0_ffn_in = {k: v for k, v in _L0_ffn_all.items() if k in ('enc_w', 'enc_b', 'sw_w', 'sw_b', 'w1', 'b1', 'w2', 'b2')}
    del _L0_ffn_all
    return {'x': x, 'adj': adj, 'L0_gnn_Wl': _L0_gnn_in['Wl'], 'L0_gnn_bl': _L0_gnn_in['bl'], 'L0_gnn_Ws': _L0_gnn_in['Ws'], 'L0_gnn_bs': _L0_gnn_in['bs'], 'L0_gnn_Wr': _L0_gnn_in['Wr'], 'L0_gnn_br': _L0_gnn_in['br'], 'L0_gnn_ln_w': _L0_gnn_in['ln_w'], 'L0_gnn_ln_b': _L0_gnn_in['ln_b'], 'L0_ffn_enc_w': _L0_ffn_in['enc_w'], 'L0_ffn_enc_b': _L0_ffn_in['enc_b'], 'L0_ffn_sw_w': _L0_ffn_in['sw_w'], 'L0_ffn_sw_b': _L0_ffn_in['sw_b'], 'L0_ffn_w1': _L0_ffn_in['w1'], 'L0_ffn_b1': _L0_ffn_in['b1'], 'L0_ffn_w2': _L0_ffn_in['w2'], 'L0_ffn_b2': _L0_ffn_in['b2']}

def reference(x, adj, L0_gnn_Wl, L0_gnn_bl, L0_gnn_Ws, L0_gnn_bs, L0_gnn_Wr, L0_gnn_br, L0_gnn_ln_w, L0_gnn_ln_b, L0_ffn_enc_w, L0_ffn_enc_b, L0_ffn_sw_w, L0_ffn_sw_b, L0_ffn_w1, L0_ffn_b1, L0_ffn_w2, L0_ffn_b2):
    import jax
    import jax.numpy as jnp

    def _L0_gnn_ref(hidden_state, adjacency_matrix, Wl, bl, Ws, bs, Wr, br, ln_w, ln_b):
        import jax, jax.numpy as jnp
        import numpy as np
        LN_EPS = 1e-12

        def _digcn_forward(hidden_state, adjacency_matrix, Wl, bl, Ws, bs, Wr, br, ln_w, ln_b):
            B, S, D = hidden_state.shape
            temper = jnp.asarray(D, jnp.float32) ** 0.5
            i = jnp.arange(S)
            upper = (i[None, :] > i[:, None]).astype(hidden_state.dtype)
            lower = (i[None, :] < i[:, None]).astype(hidden_state.dtype)

            def layer(h, params):
                wl, b_l, ws, b_s, wr, b_r, g, beta = params
                u = jnp.einsum('bid,bjd->bij', h, h) / temper
                a = jax.nn.softmax(u, axis=-1)
                delta = a * adjacency_matrix
                attn = delta / (jnp.sum(delta, axis=-1, keepdims=True) + 1e-10)
                hl = h @ wl.T + b_l
                hs = h @ ws.T + b_s
                hr = h @ wr.T + b_r
                diag_a = jnp.diagonal(attn, axis1=1, axis2=2)
                ctx = jnp.einsum('bij,bjd->bid', attn * upper, hl) + diag_a[..., None] * hs + jnp.einsum('bij,bjd->bid', attn * lower, hr)
                mean = ctx.mean(-1, keepdims=True)
                var = ctx.var(-1, keepdims=True)
                o = (ctx - mean) / jnp.sqrt(var + LN_EPS) * g + beta
                return (jax.nn.relu(o), None)
            out, _ = jax.lax.scan(layer, hidden_state, (Wl, bl, Ws, bs, Wr, br, ln_w, ln_b))
            return out
        return _digcn_forward(hidden_state, adjacency_matrix, Wl, bl, Ws, bs, Wr, br, ln_w, ln_b)

    def _L0_ffn_ref(x, enc_w, enc_b, sw_w, sw_b, w1, b1, w2, b2):
        import jax, jax.numpy as jnp
        import numpy as np
        H = 384
        R = 64
        E = 8
        B, S = (8, 1024)
        b, s, d = x.shape
        xt = x.reshape(-1, d)
        x_enc = xt @ enc_w + enc_b
        route_prob = jax.nn.softmax(x_enc @ sw_w + sw_b, axis=-1)
        route_prob_max = jnp.max(route_prob, axis=-1)
        routes = jnp.argmax(route_prob, axis=-1)
        onehot = jax.nn.one_hot(routes, E, dtype=xt.dtype)
        h = jnp.einsum('td,edr->ter', xt, w1) + b1[None]
        h = jax.nn.gelu(h, approximate=False)
        h = h * onehot[..., None]
        out = jnp.einsum('ter,erd->td', h, w2) + onehot @ b2
        out = out * route_prob_max[:, None]
        return out.reshape(b, s, d)
    x = x + _L0_gnn_ref(_layernorm(x, axis=-1), adj, L0_gnn_Wl, L0_gnn_bl, L0_gnn_Ws, L0_gnn_bs, L0_gnn_Wr, L0_gnn_br, L0_gnn_ln_w, L0_gnn_ln_b)
    x = x + _L0_ffn_ref(_layernorm(x, axis=-1), L0_ffn_enc_w, L0_ffn_enc_b, L0_ffn_sw_w, L0_ffn_sw_b, L0_ffn_w1, L0_ffn_b1, L0_ffn_w2, L0_ffn_b2)
    return x

_drawn_inputs = setup_inputs


def setup_inputs(seed=0):
    import zlib

    import numpy as np

    out = dict(_drawn_inputs(seed))
    spreads = {'L0_gnn_bl': (0.0, 0.1),
     'L0_gnn_bs': (0.0, 0.415),
     'L0_gnn_br': (0.0, 0.1),
     'L0_gnn_ln_w': (1.0, 0.2),
     'L0_gnn_ln_b': (0.0, 0.1)}
    factors = {'L0_ffn_enc_b': 8.0, 'L0_ffn_sw_b': 3.521, 'L0_ffn_b1': 31.552, 'L0_ffn_b2': 5.045}
    for name, (base, spread) in spreads.items():
        noise = np.random.default_rng([zlib.crc32(name.encode()), seed]).standard_normal(out[name].shape)
        drawn = base * np.exp(spread * noise) if base else spread * noise
        out[name] = jnp.asarray(drawn.astype(out[name].dtype))
    for name, factor in factors.items():
        out[name] = (out[name] * factor).astype(out[name].dtype)
    return out
```

```python
from contextlib import ExitStack

import numpy as np

import concourse.bass as bass
from concourse import mybir

F32 = mybir.dt.float32
F32R = mybir.dt.float32r
ALU = mybir.AluOpType
ACT = mybir.ActivationFunctionType
AX_X = mybir.AxisListType.X

P = 128
LN_INPUT_EPS = 1e-5
LN_LAYER_EPS = 1e-12
DENOM_EPS = 1e-10
SWITCHED_OFF = float(2 ** 40)
SPLIT = 32


def build(nc, x, adj, Wl, bl, Ws, bs, Wr, br, ln_w, ln_b,
          enc_w, enc_b, sw_w, sw_b, w1, b1, w2, b2, out):
    B, S, D = x.shape
    L = Wl.shape[0]
    C = D // P
    E, _, R = w1.shape
    Q = E * R // P
    G = 4
    NG = B // G
    TOK = G * P
    assert S == P and D == C * P and L == 2 and E * R == Q * P and TOK == 512 and NG % 2 == 0 and B >= 8

    ctx = ExitStack()
    with ctx:
        def sb(name, shape, dt=F32, where=ctx):
            return where.enter_context(nc.sbuf_tensor(name, shape, dt))

        def sem(name):
            return ctx.enter_context(nc.semaphore(name))

        def per_layer(name):
            return [sem(f"{name}{l}") for l in range(L)]

        x1_dram = nc.dram_tensor("x1_scratch", [B, S, D], F32, kind="Internal").ap()
        bank = [ctx.enter_context(nc.psum_tensor(f"bank{k}", [P, 512], F32)) for k in range(8)]

        ident = sb("ident", [P, P])
        ident_r = sb("ident_r", [P, P], F32R)
        minus_half = sb("minus_half", [P, G])
        w1_hi = sb("w1_hi", [P, C, E * R], F32R)
        w1_lo = sb("w1_lo", [P, C, E * R], F32R)
        w2_hi = sb("w2_hi", [P, Q, D], F32R)
        w2_lo = sb("w2_lo", [P, Q, D], F32R)
        b1_col = sb("b1_col", [P, Q])
        route_w = sb("route_w", [P, C, P], F32R)
        route_b = sb("route_b", [P, E])
        b2_rows = sb("b2_rows", [SPLIT + E, D], F32R)
        switch_off = sb("switch_off", [SPLIT + E, Q, P], F32R)

        weights_ctx = ctx.enter_context(ExitStack())
        wT_hi = sb("wT_hi", [P, L, 3, C, D], F32R, weights_ctx)
        wT_lo = sb("wT_lo", [P, L, 3, C, D], F32R, weights_ctx)
        BK = 2 * SPLIT + 3
        bias_rows = sb("bias_rows", [BK, L, D], F32R, weights_ctx)
        gamma = sb("gamma", [P, L, D], F32, weights_ctx)
        beta = sb("beta", [P, L, D], F32, weights_ctx)
        pack = [sb(f"pack{l}", [P, P], F32R, weights_ctx) for l in range(L)]

        setup_ctx = ExitStack()
        with setup_ctx:
            stage = sb("stage", [P, 3, L, C, D], F32, setup_ctx)
            w1_in = sb("w1_in", [P, C, E * R], F32, setup_ctx)
            w2_in = sb("w2_in", [P, Q, D], F32, setup_ctx)
            bias_in = sb("bias_in", [BK, L, D], F32, setup_ctx)
            b2_in = sb("b2_in", [SPLIT + E, D], F32, setup_ctx)
            b2_hi = sb("b2_hi", [SPLIT + E, D], F32R, setup_ctx)
            bias_hi = sb("bias_hi", [BK, L, D], F32R, setup_ctx)
            enc_in = sb("enc_in", [P, C, R], F32, setup_ctx)
            encT = sb("encT", [R, C, P], F32, setup_ctx)
            sw_in = sb("sw_in", [R, E], F32, setup_ctx)
            encb_col = sb("encb_col", [R, 1], F32, setup_ctx)
            encb_wide = sb("encb_wide", [R, P], F32, setup_ctx)
            swb_all = sb("swb_all", [P, E], F32, setup_ctx)
            ones = sb("ones", [R, P], F32, setup_ctx)

            ffn_in, wt_in, const_in = sem("ffn_in"), sem("wt_in"), sem("const_in")
            zeroed, ident_made, ident_r_made = sem("zeroed"), sem("ident_made"), sem("ident_r_made")
            off_filled, off_made = sem("off_filled"), sem("off_made")
            wT_done, wT_hi_made, wT_lo_made = sem("wT_done"), sem("wT_hi_made"), sem("wT_lo_made")
            split_hi = sem("split_hi")
            encT_done, encT_made, encb_made = sem("encT_done"), sem("encT_made"), sem("encb_made")
            route_done, route_hi_made, setup_end = sem("route_done"), sem("route_hi_made"), sem("setup_end")
            bias_zeroed = sem("bias_zeroed")

            FFN_LOADS, CONST_LOADS = C + 1, 18

            with nc.Block() as block:
                @block.sync
                def _(sp):
                    for m, w in enumerate((Wl, Ws, Wr)):
                        sp.dma_start(stage[:, m, :, :, :],
                                     w.rearrange("l (c p) d -> p l c d", p=P)).then_inc(wt_in, 16)
                    for c in range(C):
                        sp.dma_start(w1_in[:, c, :].rearrange("p (e r) -> p e r", e=E),
                                     w1[:, c * P:(c + 1) * P, :].rearrange("e p r -> p e r")).then_inc(ffn_in, 16)
                    sp.dma_start(w2_in[:], w2.rearrange("e r d -> (e r) d").rearrange("(q p) d -> p q d", p=P)
                                 ).then_inc(ffn_in, 16)
                    sp.dma_start(gamma[:], ln_w.partition_broadcast(P)).then_inc(const_in, 16)
                    sp.dma_start(beta[:], ln_b.partition_broadcast(P)).then_inc(const_in, 16)
                    sp.dma_start(enc_in[:], enc_w.rearrange("(c p) r -> p c r", p=P)).then_inc(const_in, 16)
                    sp.dma_start(sw_in[:], sw_w).then_inc(const_in, 16)
                    sp.dma_start(encb_col[:], enc_b.rearrange("(r a) -> r a", a=1)).then_inc(const_in, 16)
                    sp.dma_start(swb_all[:], sw_b.partition_broadcast(P)).then_inc(const_in, 16)
                    sp.dma_start(b1_col[:], b1.rearrange("e r -> (e r)").rearrange("(q p) -> p q", p=P),
                                 allow_slow_non_contiguous=True).then_inc(const_in, 16)
                    sp.wait_ge(bias_zeroed, 2)
                    for row in (0, SPLIT):
                        sp.dma_start(b2_in[row:row + E, :], b2).then_inc(const_in, 16)
                    for row, b in enumerate((bl, bs, br)):
                        for part in range(3):
                            r0 = part * SPLIT + row
                            sp.dma_start(bias_in[r0:r0 + 1, :, :], b.rearrange("(a l) d -> a l d", a=1)
                                         ).then_inc(const_in, 16)

                @block.gpsimd
                def _(pool):
                    pool.memset(bias_in[:], 0.0).then_inc(bias_zeroed, 1)
                    pool.memset(b2_in[:], 0.0).then_inc(bias_zeroed, 1)
                    pool.memset(ident[:], 0.0).then_inc(zeroed, 1)
                    pool.wait_ge(zeroed, 1)
                    pool.nop(nofuse=True)
                    pool.affine_select(out=ident[:], in_=ident[:], compare_op=ALU.not_equal, fill=1.0,
                                       base=0, pattern=[[-1, P]], channel_multiplier=1).then_inc(ident_made, 1)
                    pool.memset(minus_half[:], -0.5)

                @block.tensor
                def _(pe):
                    pe.wait_ge(ident_made, 1)
                    pe.wait_ge(wt_in, 16 * 3)
                    n = 0
                    for l in range(L):
                        for m in range(3):
                            for dc in range(C):
                                if n >= 2:
                                    pe.wait_ge(wT_lo_made, n - 1)
                                for oc in range(C):
                                    last = pe.transpose(bank[n % 2][:, oc * P:(oc + 1) * P],
                                                        stage[:, m, l, oc, dc * P:(dc + 1) * P], ident[:])
                                last.then_inc(wT_done, 1)
                                n += 1
                    pe.wait_ge(const_in, 16 * CONST_LOADS)
                    for c in range(C):
                        last = pe.transpose(bank[2][0:R, c * P:(c + 1) * P], enc_in[:, c, :], ident[:])
                    last.then_inc(encT_done, 1)
                    pe.wait_ge(encT_made, 1)
                    pe.wait_ge(encb_made, 1)
                    for c in range(C):
                        pe.matmul(bank[3][:, c * E:(c + 1) * E], encT[:, c, :], sw_in[:], start=True, stop=True)
                    pe.matmul(bank[3][:, C * E:(C + 1) * E], encb_wide[:], sw_in[:],
                              start=True, stop=True).then_inc(route_done, 1)

                @block.scalar
                def _(act):
                    n = 0
                    for l in range(L):
                        for m in range(3):
                            for dc in range(C):
                                act.wait_ge(wT_done, n + 1)
                                act.copy(wT_hi[:, l, m, dc, :], bank[n % 2][:, 0:D]).then_inc(wT_hi_made, 1)
                                n += 1
                    act.wait_ge(ffn_in, 16 * FFN_LOADS)
                    act.copy(w1_hi[:], w1_in[:]).then_inc(split_hi, 1)
                    act.copy(w2_hi[:], w2_in[:]).then_inc(split_hi, 1)
                    act.wait_ge(encT_done, 1)
                    act.copy(encT[:], bank[2][0:R, 0:C * P].rearrange("r (c p) -> r c p", c=C)
                             ).then_inc(encT_made, 1)

                @block.vector
                def _(dve):
                    dve.memset(switch_off[:].bitcast(F32), 0.0)
                    dve.memset(route_w[:].bitcast(F32), 0.0)
                    for l in range(L):
                        dve.memset(pack[l][:].bitcast(F32), 0.0)
                    dve.memset(bias_rows[:].bitcast(F32), 0.0)
                    dve.memset(b2_rows[:].bitcast(F32), 0.0)
                    dve.memset(ones[:], 1.0).then_inc(off_filled, 1)
                    dve.wait_ge(ident_made, 1)
                    dve.tensor_copy(ident_r[:], ident[:]).then_inc(ident_r_made, 1)
                    dve.wait_ge(off_filled, 1)
                    dve.tensor_scalar(switch_off[0:E, :, :].rearrange("k q (h r) -> k (q h) r", h=P // R),
                                      ident[0:E, 0:E].unsqueeze(2).broadcast_to([E, E, R]),
                                      SWITCHED_OFF, -SWITCHED_OFF, ALU.mult, ALU.add).then_inc(off_made, 1)
                    n = 0
                    for l in range(L):
                        for m in range(3):
                            for dc in range(C):
                                dve.wait_ge(wT_hi_made, n + 1)
                                dve.tensor_tensor(wT_lo[:, l, m, dc, :], bank[n % 2][:, 0:D],
                                                  wT_hi[:, l, m, dc, :].bitcast(F32),
                                                  ALU.subtract).then_inc(wT_lo_made, 1)
                                n += 1
                    dve.wait_ge(split_hi, 2)
                    dve.tensor_tensor(w1_lo[:], w1_in[:], w1_hi[:].bitcast(F32), ALU.subtract)
                    dve.tensor_tensor(w2_lo[:], w2_in[:], w2_hi[:].bitcast(F32), ALU.subtract)
                    dve.wait_ge(const_in, 16 * CONST_LOADS)
                    dve.tensor_copy(bias_hi[:], bias_in[:]).then_inc(split_hi, 1)
                    dve.tensor_copy(b2_hi[:], b2_in[:]).then_inc(split_hi, 1)
                    dve.wait_ge(split_hi, 4)
                    for part in (0, 2):
                        dve.tensor_copy(bias_rows[part * SPLIT:part * SPLIT + 3, :, :],
                                        bias_hi[part * SPLIT:part * SPLIT + 3, :, :].bitcast(F32))
                    dve.tensor_tensor(bias_rows[SPLIT:SPLIT + 3, :, :], bias_in[SPLIT:SPLIT + 3, :, :],
                                      bias_hi[SPLIT:SPLIT + 3, :, :].bitcast(F32), ALU.subtract)
                    dve.tensor_copy(b2_rows[0:E, :], b2_hi[0:E, :].bitcast(F32))
                    dve.tensor_tensor(b2_rows[SPLIT:SPLIT + E, :], b2_in[SPLIT:SPLIT + E, :],
                                      b2_hi[SPLIT:SPLIT + E, :].bitcast(F32), ALU.subtract)
                    dve.tensor_scalar(encb_wide[:], ones[:], encb_col[:, 0:1], None, ALU.mult
                                      ).then_inc(encb_made, 1)
                    dve.wait_ge(route_done, 1)
                    dve.tensor_copy(route_w[:, :, 0:E], bank[3][:, 0:C * E].rearrange("p (c e) -> p c e", c=C)
                                    ).then_inc(route_hi_made, 1)
                    dve.wait_ge(route_hi_made, 1)
                    dve.tensor_tensor(route_w[:, :, SPLIT:SPLIT + E],
                                      bank[3][:, 0:C * E].rearrange("p (c e) -> p c e", c=C),
                                      route_w[:, :, 0:E].bitcast(F32), ALU.subtract)
                    dve.tensor_tensor(route_b[:], bank[3][:, C * E:(C + 1) * E], swb_all[:], ALU.add)

        gnn_ctx = ExitStack()
        with gnn_ctx:
            def per_layer_sb(name, shape, dt=F32):
                return [sb(f"{name}{l}", shape, dt, gnn_ctx) for l in range(L)]

            x_in = sb("x_in", [P, D], F32, gnn_ctx)
            x_res = sb("x_res", [P, D], F32, gnn_ctx)
            x1_out = sb("x1_out", [P, D], F32, gnn_ctx)
            relu_out = sb("relu_out", [P, D], F32, gnn_ctx)
            adj_in = per_layer_sb("adj_in", [P, P])
            masks = per_layer_sb("masks", [P, 3, P])
            h = per_layer_sb("h", [P, D])
            h_hi = per_layer_sb("h_hi", [P, D], F32R)
            h_lo = per_layer_sb("h_lo", [P, D], F32R)
            hT = per_layer_sb("hT", [P, D])
            hT_hi = per_layer_sb("hT_hi", [P, D], F32R)
            hT_lo = per_layer_sb("hT_lo", [P, D], F32R)
            expo = sb("expo", [P, P], F32, gnn_ctx)
            delta = sb("delta", [P, 3, P], F32, gnn_ctx)
            deltaT_hi = sb("deltaT_hi", [P, 2 * P], F32R, gnn_ctx)
            deltaT_lo = sb("deltaT_lo", [P, 2 * P], F32R, gnn_ctx)
            sumsT = per_layer_sb("sumsT", [BK, P], F32R)
            agg_hi = sb("agg_hi", [P, C, 2 * P], F32R, gnn_ctx)
            agg_lo = sb("agg_lo", [P, C, 2 * P], F32R, gnn_ctx)
            self_term = per_layer_sb("self_term", [P, D])
            ctx_sb = per_layer_sb("ctx_sb", [P, D])
            normed = per_layer_sb("normed", [P, D])
            ln1_bn = sb("ln1_bn", [P, 6], F32, gnn_ctx)
            ln1_mv = sb("ln1_mv", [P, 2], F32, gnn_ctx)
            ln1_t = sb("ln1_t", [P, 1], F32, gnn_ctx)
            ln1_scale = sb("ln1_scale", [P, 1], F32, gnn_ctx)
            ln1_shift = sb("ln1_shift", [P, 1], F32, gnn_ctx)
            row_max = per_layer_sb("row_max", [P, 1])
            neg_max = per_layer_sb("neg_max", [P, 1])
            exp_sum = per_layer_sb("exp_sum", [P, 1])
            sums = per_layer_sb("sums", [P, 3])
            sum_all = per_layer_sb("sum_all", [P, 1])
            denom = per_layer_sb("denom", [P, 1])
            inv_denom = per_layer_sb("inv_denom", [P, 1])
            bn = per_layer_sb("bn", [P, 6])
            mv = per_layer_sb("mv", [P, 2])
            var_n = per_layer_sb("var_n", [P, 1])
            var_e = per_layer_sb("var_e", [P, 1])
            rstd = per_layer_sb("rstd", [P, 1])
            out_scale = per_layer_sb("out_scale", [P, 1])

            x_loaded, xres_loaded, x1_stored = sem("x_loaded"), sem("xres_loaded"), sem("x1_stored")
            adj_loaded = per_layer("adj_loaded")
            ln1_bn_done, ln1_stats_done = sem("ln1_bn_done"), sem("ln1_stats_done")
            ln1_eps_added, ln1_rstd_done, ln1_scale_ready = sem("ln1_eps_added"), sem("ln1_rstd_done"), sem("ln1_scale_ready")
            h_ready, masks_ready = per_layer("h_ready"), per_layer("masks_ready")
            hT_done, hT_ready, hThi_ready, hTlo_ready = (per_layer(n) for n in (
                "hT_done", "hT_ready", "hThi_ready", "hTlo_ready"))
            hhi_ready, hlo_ready = per_layer("hhi_ready"), per_layer("hlo_ready")
            scores_done, max_done, negmax_ready, exp_done = (per_layer(n) for n in (
                "scores_done", "max_done", "negmax_ready", "exp_done"))
            delta_ready, sums_hi_done, sums_ready = (per_layer(n) for n in (
                "delta_ready", "sums_hi_done", "sums_ready"))
            sum_done, denom_done, inv_done = (per_layer(n) for n in ("sum_done", "denom_done", "inv_done"))
            deltaT_done, deltaThi_ready, deltaTlo_ready, sumsT_ready = (per_layer(n) for n in (
                "deltaT_done", "deltaThi_ready", "deltaTlo_ready", "sumsT_ready"))
            agg_done = [[sem(f"agg_done{l}_{c}") for c in range(C)] for l in range(L)]
            agghi_ready = [[sem(f"agghi_ready{l}_{c}") for c in range(C)] for l in range(L)]
            agglo_ready = [[sem(f"agglo_ready{l}_{c}") for c in range(C)] for l in range(L)]
            self_done, self_ready, ctx_done, ctx_ready = (per_layer(n) for n in (
                "self_done", "self_ready", "ctx_done", "ctx_ready"))
            bn_done, stats_done, scaled_once, eps_added, rstd_done, scale_ready = (per_layer(n) for n in (
                "bn_done", "stats_done", "scaled_once", "eps_added", "rstd_done", "scale_ready"))
            centred, tail_done = per_layer("centred"), per_layer("tail_done")
            relu_done, x1_ready = sem("relu_done"), sem("x1_ready")

            hT_bank, score_bank, deltaT_bank, self_bank, ctx_bank = bank[0], bank[1], bank[2], bank[3], bank[4]
            agg_bank = bank[5:8]

            def unit(s, l):
                return None if isinstance(s, int) and not 0 <= s < B else (s, l)

            def half_steps(i):
                return ((unit(i, 0), unit(i - 2, 1), unit(i - 1, 0), unit(i - 1, 1)),
                        (unit(i - 1, 1), unit(i, 0), unit(i - 2, 1), unit(i + 1, 0)))

            def before(s, l):
                if l == 0:
                    return unit(s - 2, 1) or unit(s - 1, 0)
                return unit(s + 1, 0) or unit(s - 1, 1)

            FIRST, LAST = 3, B - 2

            def steps(eng, step):
                for i in range(FIRST):
                    step(i)
                with eng.Fori(FIRST, LAST + 1) as i:
                    step(i)
                for i in range(LAST + 1, B + 3):
                    step(i)

            with nc.Block() as block:
                @block.sync
                def _(sp):
                    def load_x(s):
                        if not isinstance(s, int) or s > 0:
                            sp.wait_ge(h_ready[0], s)
                        sp.dma_start(x_in[:], x[s, :, :]).then_inc(x_loaded, 16)

                    def load_adj(s, l):
                        if not isinstance(s, int) or s > 0:
                            sp.wait_ge(masks_ready[l], s)
                        sp.dma_start(adj_in[l][:], adj[s, :, :]).then_inc(adj_loaded[l], 16)

                    def load_residual(s):
                        if not isinstance(s, int) or s > 0:
                            sp.wait_ge(x1_ready, s)
                        sp.dma_start(x_res[:], x[s, :, :]).then_inc(xres_loaded, 16)

                    def step(i):
                        if unit(i + 1, 0):
                            load_x(i + 1)
                            load_adj(i + 1, 0)
                        if unit(i, 0):
                            load_adj(i, 1)
                        if unit(i - 2, 1):
                            sp.wait_ge(x1_ready, i - 1)
                            sp.dma_start(x1_dram[i - 2, :, :], x1_out[:]).then_inc(x1_stored, 16)
                        if unit(i - 1, 1):
                            load_residual(i - 1)

                    load_x(0)
                    load_adj(0, 0)
                    steps(sp, step)
                    sp.wait_ge(x1_stored, 16 * B)

                @block.tensor
                def _(pe):
                    def transposes(s, l):
                        pe.wait_ge(h_ready[l], s + 1)
                        if before(s, l):
                            sb_, lb = before(s, l)
                            pe.wait_ge(hThi_ready[lb], sb_ + 1)
                        for c in range(C):
                            last = pe.transpose(hT_bank[:, c * P:(c + 1) * P], h[l][:, c * P:(c + 1) * P], ident[:])
                        last.then_inc(hT_done[l], 1)

                    def scores(s, l):
                        pe.wait_ge(hT_ready[l], s + 1)
                        if before(s, l):
                            sb_, lb = before(s, l)
                            pe.wait_ge(exp_done[lb], sb_ + 1)
                        for c in range(C):
                            hc = hT[l][:, c * P:(c + 1) * P]
                            last = pe.matmul(score_bank[:, 0:P], hc, hc, start=(c == 0), stop=(c == C - 1))
                        last.then_inc(scores_done[l], 1)

                    def turn_delta(s, l):
                        pe.wait_ge(sums_ready[l], s + 1)
                        if before(s, l):
                            sb_, lb = before(s, l)
                            pe.wait_ge(sumsT_ready[lb], sb_ + 1)
                            pe.wait_ge(deltaTlo_ready[lb], sb_ + 1)
                        pe.transpose(deltaT_bank[:, 0:P], delta[:, 0, :], ident[:])
                        pe.transpose(deltaT_bank[:, P:2 * P], delta[:, 2, :], ident[:])
                        pe.transpose(deltaT_bank[:, 2 * P:3 * P].bitcast(F32R), pack[l][:], ident_r[:]
                                     ).then_inc(deltaT_done[l], 1)

                    def self_product(s, l, chunks):
                        if 0 in chunks:
                            pe.wait_ge(hThi_ready[l], s + 1)
                            pe.wait_ge(hTlo_ready[l], s + 1)
                            if before(s, l):
                                sb_, lb = before(s, l)
                                pe.wait_ge(self_ready[lb], sb_ + 1)
                        for c in chunks:
                            hi, lo = hT_hi[l][:, c * P:(c + 1) * P], hT_lo[l][:, c * P:(c + 1) * P]
                            w_hi, w_lo = wT_hi[:, l, 1, c, :], wT_lo[:, l, 1, c, :]
                            pe.matmul(self_bank[:, 0:D], hi, w_hi, start=(c == 0), stop=False)
                            pe.matmul(self_bank[:, 0:D], hi, w_lo, start=False, stop=False)
                            last = pe.matmul(self_bank[:, 0:D], lo, w_hi, start=False, stop=(c == C - 1))
                        if C - 1 in chunks:
                            last.then_inc(self_done[l], 1)

                    def neighbour_sums(s, l):
                        pe.wait_ge(hhi_ready[l], s + 1)
                        pe.wait_ge(hlo_ready[l], s + 1)
                        pe.wait_ge(deltaThi_ready[l], s + 1)
                        pe.wait_ge(deltaTlo_ready[l], s + 1)
                        for c in range(C):
                            if before(s, l):
                                sb_, lb = before(s, l)
                                pe.wait_ge(agglo_ready[lb][c], sb_ + 1)
                            o = agg_bank[c][:, 0:2 * P]
                            hi, lo = h_hi[l][:, c * P:(c + 1) * P], h_lo[l][:, c * P:(c + 1) * P]
                            pe.matmul(o, hi, deltaT_hi[:], start=True, stop=False)
                            pe.matmul(o, hi, deltaT_lo[:], start=False, stop=False)
                            pe.matmul(o, lo, deltaT_hi[:], start=False, stop=True).then_inc(agg_done[l][c], 1)

                    def projection(s, l, chunks):
                        if 0 in chunks and before(s, l):
                            sb_, lb = before(s, l)
                            pe.wait_ge(ctx_ready[lb], sb_ + 1)
                        for c in chunks:
                            pe.wait_ge(agghi_ready[l][c], s + 1)
                            pe.wait_ge(agglo_ready[l][c], s + 1)
                            for side in range(2):
                                hi = agg_hi[:, c, side * P:(side + 1) * P]
                                lo = agg_lo[:, c, side * P:(side + 1) * P]
                                w_hi, w_lo = wT_hi[:, l, 2 * side, c, :], wT_lo[:, l, 2 * side, c, :]
                                pe.matmul(ctx_bank[:, 0:D], hi, w_hi, start=(c == 0 and side == 0), stop=False)
                                pe.matmul(ctx_bank[:, 0:D], hi, w_lo, start=False, stop=False)
                                pe.matmul(ctx_bank[:, 0:D], lo, w_hi, start=False, stop=False)
                        if C - 1 in chunks:
                            pe.wait_ge(sumsT_ready[l], s + 1)
                            pe.matmul(ctx_bank[:, 0:D], sumsT[l][:], bias_rows[:, l, :],
                                      start=False, stop=True).then_inc(ctx_done[l], 1)

                    def step(i):
                        for front, back, _, turned in half_steps(i):
                            if back:
                                projection(*back, range(0, 1))
                            if front:
                                scores(*front)
                            if back:
                                projection(*back, range(1, C))
                            if front:
                                turn_delta(*front)
                                self_product(*front, range(0, C - 1))
                                neighbour_sums(*front)
                            if turned:
                                transposes(*turned)
                            if front:
                                self_product(*front, range(C - 1, C))

                    transposes(0, 0)
                    steps(pe, step)

                @block.scalar
                def _(act):
                    def copy_hT(s, l):
                        act.wait_ge(hT_done[l], s + 1)
                        if not isinstance(s, int) or s > 0:
                            act.wait_ge(hTlo_ready[l], s)
                            act.wait_ge(scores_done[l], s)
                            act.wait_ge(self_done[l], s)
                        act.copy(hT[l][:], hT_bank[:, 0:D]).then_inc(hT_ready[l], 1)
                        act.copy(hT_hi[l][:], hT_bank[:, 0:D]).then_inc(hThi_ready[l], 1)

                    def self_weighting(s, l):
                        act.wait_ge(self_done[l], s + 1)
                        act.wait_ge(delta_ready[l], s + 1)
                        if not isinstance(s, int) or s > 0:
                            act.wait_ge(ctx_ready[l], s)
                        act.activation(self_term[l][:], self_bank[:, 0:D], ACT.Copy,
                                       scale=sums[l][:, 1:2]).then_inc(self_ready[l], 1)

                    def relu(s, l):
                        act.wait_ge(tail_done[l], s + 1)
                        if l == 0:
                            if not isinstance(s, int) or s > 0:
                                act.wait_ge(hT_done[1], s)
                                act.wait_ge(hhi_ready[1], s)
                                act.wait_ge(hlo_ready[1], s)
                            act.activation(h[1][:], normed[0][:], ACT.Relu).then_inc(h_ready[1], 1)
                        else:
                            if not isinstance(s, int) or s > 0:
                                act.wait_ge(x1_ready, s)
                            act.activation(relu_out[:], normed[1][:], ACT.Relu).then_inc(relu_done, 1)

                    def normalise_x(s):
                        act.wait_ge(ln1_scale_ready, s + 1)
                        if not isinstance(s, int) or s > 0:
                            act.wait_ge(hT_done[0], s)
                            act.wait_ge(hhi_ready[0], s)
                            act.wait_ge(hlo_ready[0], s)
                        act.activation(h[0][:], x_in[:], ACT.Identity, bias=ln1_shift[:, 0:1],
                                       scale=ln1_scale[:, 0:1]).then_inc(h_ready[0], 1)

                    def exponentials(s, l):
                        act.wait_ge(negmax_ready[l], s + 1)
                        if before(s, l):
                            sb_, lb = before(s, l)
                            act.wait_ge(delta_ready[lb], sb_ + 1)
                        act.activation(expo[:], score_bank[:, 0:P], ACT.Exp, bias=neg_max[l][:, 0:1],
                                       scale=float(D) ** -0.5, accum_out=exp_sum[l][:, 0:1]
                                       ).then_inc(exp_done[l], 1)

                    def copy_deltaT(s, l):
                        act.wait_ge(deltaT_done[l], s + 1)
                        if not isinstance(s, int) or s > 0:
                            act.wait_ge(ctx_done[l], s)
                        act.copy(sumsT[l][:], deltaT_bank[0:BK, 2 * P:3 * P]).then_inc(sumsT_ready[l], 1)
                        if before(s, l):
                            sb_, lb = before(s, l)
                            act.wait_ge(agg_done[lb][C - 1], sb_ + 1)
                        act.copy(deltaT_hi[:], deltaT_bank[:, 0:2 * P]).then_inc(deltaThi_ready[l], 1)

                    def copy_agg(s, l):
                        if before(s, l):
                            sb_, lb = before(s, l)
                            act.wait_ge(ctx_done[lb], sb_ + 1)
                        for c in range(C):
                            act.wait_ge(agg_done[l][c], s + 1)
                            act.copy(agg_hi[:, c, :], agg_bank[c][:, 0:2 * P]).then_inc(agghi_ready[l][c], 1)

                    def step(i):
                        for half, (front, back, tail, _) in enumerate(half_steps(i)):
                            if front:
                                copy_hT(*front)
                            if back:
                                self_weighting(*back)
                            if tail:
                                relu(*tail)
                            if half == 1 and unit(i + 1, 0):
                                normalise_x(i + 1)
                            if front:
                                exponentials(*front)
                                copy_deltaT(*front)
                                copy_agg(*front)

                    normalise_x(0)
                    steps(act, step)

                @block.vector
                def _(dve):
                    def x_stats(s):
                        dve.wait_ge(x_loaded, 16 * (s + 1))
                        dve.bn_stats(ln1_bn[:], x_in[:]).then_inc(ln1_bn_done, 1)
                        dve.wait_ge(ln1_bn_done, s + 1)
                        if not isinstance(s, int) or s > 0:
                            dve.wait_ge(ln1_scale_ready, s)
                        dve.nop(nofuse=True)
                        dve.bn_aggr(ln1_mv[:], ln1_bn[:]).then_inc(ln1_stats_done, 1)

                    def split_h(s, l):
                        dve.wait_ge(h_ready[l], s + 1)
                        if not isinstance(s, int) or s > 0:
                            dve.wait_ge(agg_done[l][C - 1], s)
                            dve.wait_ge(hlo_ready[l], s)
                        dve.tensor_copy(h_hi[l][:], h[l][:]).then_inc(hhi_ready[l], 1)

                    def row_maximum(s, l):
                        dve.wait_ge(scores_done[l], s + 1)
                        dve.tensor_reduce(row_max[l][:], score_bank[:, 0:P], AX_X, ALU.max).then_inc(max_done[l], 1)
                        dve.wait_ge(max_done[l], s + 1)
                        dve.tensor_scalar(neg_max[l][:], row_max[l][:], -float(D) ** -0.5, None,
                                          ALU.mult).then_inc(negmax_ready[l], 1)

                    def masked_sums(s, l):
                        dve.wait_ge(exp_done[l], s + 1)
                        dve.wait_ge(masks_ready[l], s + 1)
                        if before(s, l):
                            sb_, lb = before(s, l)
                            dve.wait_ge(deltaT_done[lb], sb_ + 1)
                        for side in range(3):
                            last = dve.tensor_tensor_reduce(delta[:, side, :], expo[:], masks[l][:, side, :],
                                                            1.0, 0.0, ALU.mult, ALU.add, sums[l][:, side:side + 1])
                        last.then_inc(delta_ready[l], 1)

                    def pack_sums(s, l):
                        dve.wait_ge(delta_ready[l], s + 1)
                        if not isinstance(s, int) or s > 0:
                            dve.wait_ge(deltaT_done[l], s)
                        dve.tensor_copy(pack[l][:, 0:2 * SPLIT].rearrange("p (a b) -> p a b", a=2)[:, :, 0:3],
                                        sums[l][:].unsqueeze(1).broadcast_to([P, 2, 3])
                                        ).then_inc(sums_hi_done[l], 1)
                        dve.scalar_tensor_tensor(sum_all[l][:], sums[l][:, 0:1], sums[l][:, 1:2], sums[l][:, 2:3],
                                                 ALU.add, ALU.add).then_inc(sum_done[l], 1)
                        dve.wait_ge(sums_hi_done[l], s + 1)
                        dve.tensor_tensor(pack[l][:, 2 * SPLIT:BK], sums[l][:], pack[l][:, 0:3].bitcast(F32),
                                          ALU.subtract).then_inc(sums_ready[l], 1)

                    def denominator(s, l):
                        dve.wait_ge(sum_done[l], s + 1)
                        dve.scalar_tensor_tensor(denom[l][:], exp_sum[l][:], DENOM_EPS, sum_all[l][:],
                                                 ALU.mult, ALU.add).then_inc(denom_done[l], 1)

                    def inverse(s, l):
                        dve.wait_ge(denom_done[l], s + 1)
                        if not isinstance(s, int) or s > 0:
                            dve.wait_ge(scale_ready[l], s)
                        dve.reciprocal(inv_denom[l][:], denom[l][:]).then_inc(inv_done[l], 1)

                    def add_self(s, l):
                        dve.wait_ge(ctx_done[l], s + 1)
                        dve.wait_ge(self_ready[l], s + 1)
                        dve.tensor_tensor(ctx_sb[l][:], ctx_bank[:, 0:D], self_term[l][:], ALU.add
                                          ).then_inc(ctx_ready[l], 1)

                    def ctx_stats(s, l):
                        dve.wait_ge(ctx_ready[l], s + 1)
                        dve.bn_stats(bn[l][:], ctx_sb[l][:]).then_inc(bn_done[l], 1)

                    def ctx_moments(s, l):
                        dve.wait_ge(bn_done[l], s + 1)
                        dve.nop(nofuse=True)
                        dve.bn_aggr(mv[l][:], bn[l][:]).then_inc(stats_done[l], 1)

                    def centre(s, l):
                        dve.wait_ge(stats_done[l], s + 1)
                        if not isinstance(s, int) or s > 0:
                            dve.wait_ge(h_ready[1] if l == 0 else relu_done, s)
                        dve.scalar_tensor_tensor(normed[l][:], ctx_sb[l][:], mv[l][:, 0:1], gamma[:, l, :],
                                                 ALU.subtract, ALU.mult).then_inc(centred[l], 1)

                    def scale_shift(s, l):
                        dve.wait_ge(scale_ready[l], s + 1)
                        dve.wait_ge(centred[l], s + 1)
                        dve.scalar_tensor_tensor(normed[l][:], normed[l][:], out_scale[l][:, 0:1], beta[:, l, :],
                                                 ALU.mult, ALU.add).then_inc(tail_done[l], 1)

                    def deltaT_low(s, l):
                        dve.wait_ge(deltaThi_ready[l], s + 1)
                        dve.tensor_tensor(deltaT_lo[:], deltaT_bank[:, 0:2 * P], deltaT_hi[:].bitcast(F32),
                                          ALU.subtract).then_inc(deltaTlo_ready[l], 1)

                    def agg_low(s, l):
                        for c in range(C):
                            dve.wait_ge(agghi_ready[l][c], s + 1)
                            dve.tensor_tensor(agg_lo[:, c, :], agg_bank[c][:, 0:2 * P],
                                              agg_hi[:, c, :].bitcast(F32), ALU.subtract
                                              ).then_inc(agglo_ready[l][c], 1)

                    def step(i):
                        for half, (front, back, tail, _) in enumerate(half_steps(i)):
                            if front:
                                split_h(*front)
                            if tail:
                                scale_shift(*tail)
                            if front:
                                row_maximum(*front)
                            if half == 0 and unit(i + 1, 0):
                                x_stats(i + 1)
                            if front:
                                masked_sums(*front)
                                pack_sums(*front)
                                denominator(*front)
                            if back:
                                add_self(*back)
                            if front:
                                inverse(*front)
                                deltaT_low(*front)
                            if back:
                                ctx_stats(*back)
                                ctx_moments(*back)
                            if front:
                                agg_low(*front)
                            if back:
                                centre(*back)

                    x_stats(0)
                    steps(dve, step)

                @block.gpsimd
                def _(pool):
                    def split_hT(s, l):
                        pool.wait_ge(hThi_ready[l], s + 1)
                        pool.tensor_tensor(hT_lo[l][:], hT[l][:], hT_hi[l][:].bitcast(F32), ALU.subtract
                                           ).then_inc(hTlo_ready[l], 1)

                    def split_h(s, l):
                        pool.wait_ge(hhi_ready[l], s + 1)
                        pool.tensor_tensor(h_lo[l][:], h[l][:], h_hi[l][:].bitcast(F32), ALU.subtract
                                           ).then_inc(hlo_ready[l], 1)

                    def residual(s):
                        pool.wait_ge(relu_done, s + 1)
                        pool.wait_ge(xres_loaded, 16 * (s + 1))
                        if not isinstance(s, int) or s > 0:
                            pool.wait_ge(x1_stored, 16 * s)
                        pool.tensor_tensor(x1_out[:], relu_out[:], x_res[:], ALU.add).then_inc(x1_ready, 1)

                    def make_masks(s, l):
                        pool.wait_ge(adj_loaded[l], 16 * (s + 1))
                        if not isinstance(s, int) or s > 0:
                            pool.wait_ge(delta_ready[l], s)
                        pool.nop(nofuse=True)
                        pool.affine_select(out=masks[l][:, 0, :], in_=adj_in[l][:], compare_op=ALU.is_gt, fill=0.0,
                                           base=0, pattern=[[1, P]], channel_multiplier=-1)
                        pool.affine_select(out=masks[l][:, 1, :], in_=adj_in[l][:], compare_op=ALU.is_equal,
                                           fill=0.0, base=0, pattern=[[1, P]], channel_multiplier=-1)
                        pool.affine_select(out=masks[l][:, 2, :], in_=adj_in[l][:], compare_op=ALU.is_gt, fill=0.0,
                                           base=0, pattern=[[-1, P]], channel_multiplier=1
                                           ).then_inc(masks_ready[l], 1)

                    def layer_scale(s, l):
                        pool.wait_ge(stats_done[l], s + 1)
                        pool.wait_ge(inv_done[l], s + 1)
                        if not isinstance(s, int) or s > 0:
                            pool.wait_ge(tail_done[l], s)
                        pool.nop(nofuse=True)
                        pool.tensor_scalar(var_n[l][:], mv[l][:, 1:2], inv_denom[l][:, 0:1], inv_denom[l][:, 0:1],
                                           ALU.mult, ALU.mult).then_inc(scaled_once[l], 1)
                        pool.wait_ge(scaled_once[l], s + 1)
                        pool.nop(nofuse=True)
                        pool.tensor_scalar(var_e[l][:], var_n[l][:], LN_LAYER_EPS, None, ALU.add
                                           ).then_inc(eps_added[l], 1)
                        pool.wait_ge(eps_added[l], s + 1)
                        pool.tensor_tensor(rstd[l][:], var_e[l][:], minus_half[:, 0:1], ALU.pow
                                           ).then_inc(rstd_done[l], 1)
                        pool.wait_ge(rstd_done[l], s + 1)
                        pool.tensor_tensor(out_scale[l][:], rstd[l][:], inv_denom[l][:], ALU.mult
                                           ).then_inc(scale_ready[l], 1)

                    def x_scale(s):
                        pool.wait_ge(ln1_stats_done, s + 1)
                        if not isinstance(s, int) or s > 0:
                            pool.wait_ge(h_ready[0], s)
                        pool.nop(nofuse=True)
                        pool.tensor_scalar(ln1_t[:], ln1_mv[:, 1:2], LN_INPUT_EPS, None, ALU.add
                                           ).then_inc(ln1_eps_added, 1)
                        pool.wait_ge(ln1_eps_added, s + 1)
                        pool.tensor_tensor(ln1_scale[:], ln1_t[:], minus_half[:, 0:1], ALU.pow
                                           ).then_inc(ln1_rstd_done, 1)
                        pool.wait_ge(ln1_rstd_done, s + 1)
                        pool.nop(nofuse=True)
                        pool.tensor_scalar(ln1_shift[:], ln1_mv[:, 0:1], ln1_scale[:, 0:1], -1.0,
                                           ALU.mult, ALU.mult).then_inc(ln1_scale_ready, 1)

                    def step(i):
                        for half, (front, back, tail, turned) in enumerate(half_steps(i)):
                            if front:
                                split_hT(*front)
                                split_h(*front)
                            if tail and tail[1] == 1:
                                residual(tail[0])
                            if half == 0 and unit(i + 1, 0):
                                x_scale(i + 1)
                            if turned:
                                make_masks(*turned)
                            if back:
                                layer_scale(*back)

                    x_scale(0)
                    make_masks(0, 0)
                    steps(pool, step)

        weights_ctx.close()

        ffn_ctx = ExitStack()
        with ffn_ctx:
            def pair(name, shape, dt=F32):
                return [sb(f"{name}{k}", shape, dt, ffn_ctx) for k in range(2)]

            ROUTE = SPLIT + E
            x1 = pair("x1_", [P, G, D])
            oneT = pair("oneT", [ROUTE, TOK], F32R)
            top_prob = pair("top_prob", [P, G])
            out_sb = pair("out_sb", [P, G, D])
            n2 = sb("n2", [P, G, D], F32, ffn_ctx)
            n2T_hi = sb("n2T_hi", [P, C, TOK], F32R, ffn_ctx)
            n2T_lo = sb("n2T_lo", [P, C, TOK], F32R, ffn_ctx)
            gelu_out = sb("gelu_out", [P, Q, TOK], F32, ffn_ctx)
            gelu_hi = sb("gelu_hi", [P, Q, TOK], F32R, ffn_ctx)
            gelu_lo = sb("gelu_lo", [P, Q, TOK], F32R, ffn_ctx)
            bn2 = sb("bn2", [P, G, 6], F32, ffn_ctx)
            mv2 = sb("mv2", [P, G, 2], F32, ffn_ctx)
            var2 = sb("var2", [P, G], F32, ffn_ctx)
            scale2 = sb("scale2", [P, G], F32, ffn_ctx)
            shift2a = sb("shift2a", [P, G], F32, ffn_ctx)
            shift2 = sb("shift2", [P, G], F32, ffn_ctx)
            minus_one = sb("minus_one", [P, G], F32, ffn_ctx)
            euler = sb("euler", [P, G, E], F32, ffn_ctx)
            rank = sb("rank", [P, G, E], F32, ffn_ctx)
            logitsT = sb("logitsT", [ROUTE, TOK], F32, ffn_ctx)
            parts = sb("parts", [P, G, ROUTE], F32, ffn_ctx)
            raw = sb("raw", [P, G, E], F32, ffn_ctx)
            logits = sb("logits", [P, G, E], F32, ffn_ctx)
            top = sb("top", [P, G], F32, ffn_ctx)
            is_top = sb("is_top", [P, G, E], F32, ffn_ctx)
            key = sb("key", [P, G, E], F32, ffn_ctx)
            best = sb("best", [P, G], F32, ffn_ctx)
            one_hot = sb("one_hot", [P, G, ROUTE], F32R, ffn_ctx)
            below_top = sb("below_top", [P, G, E], F32, ffn_ctx)
            odds = sb("odds", [P, G, E], F32, ffn_ctx)
            odds_sum = sb("odds_sum", [P, G], F32, ffn_ctx)

            names = ("bn2_done mv2_done var2_done scale2_done shift2a_done shift2_done n2_ready "
                     "consts_made rank_base one_hot_zeroed logitsT_done logitsT_ready parts_done parts_ready raw_done "
                     "logits_done top_done below_done odds_ready odds_sum_done prob_ready is_top_done "
                     "key_done best_done one_hot_ready oneT_done oneT_ready").split()
            (bn2_done, mv2_done, var2_done, scale2_done, shift2a_done, shift2_done, n2_ready,
             consts_made, rank_base, one_hot_zeroed, logitsT_done, logitsT_ready, parts_done, parts_ready, raw_done,
             logits_done, top_done, below_done, odds_ready, odds_sum_done, prob_ready, is_top_done,
             key_done, best_done, one_hot_ready, oneT_done, oneT_ready) = map(sem, names)
            x1_loaded, out_stored = ([sem(f"{n}_{k}") for k in range(2)] for n in ("x1_loaded", "out_stored"))
            n2T_done, n2Thi_ready, n2Tlo_ready = map(sem, ("n2T_done", "n2Thi_ready", "n2Tlo_ready"))
            hidden_done, gelu_ready, geluhi_ready, gelulo_ready = map(sem, (
                "hidden_done", "gelu_ready", "geluhi_ready", "gelulo_ready"))
            y_done, y_ready = map(sem, ("y_done", "y_ready"))

            n2T_bank = (bank[0], bank[1], bank[0])
            logitsT_bank, small_bank = bank[2], bank[3]
            hidden_bank = (bank[4], bank[5])
            y_bank = (bank[6], bank[7])

            x1_groups = x1_dram.rearrange("(g t) p d -> g p t d", t=G)
            out_groups = out.rearrange("(g t) p d -> g p t d", t=G)

            def there(g):
                return not isinstance(g, int) or g < NG

            def groups(eng, group):
                for g in range(2):
                    group(g, g)
                with eng.Fori(1, NG // 2 - 1) as i:
                    for k in range(2):
                        group(i * 2 + k, k)
                for g in range(NG - 2, NG):
                    group(g, g % 2)

            with nc.Block() as block:
                @block.sync
                def _(sp):
                    def load(g, k):
                        if not isinstance(g, int) or g > 1:
                            sp.wait_ge(y_ready, G * (g - 1))
                        sp.dma_start(x1[k][:], x1_groups[g, :, :, :]).then_inc(x1_loaded[k], 16)

                    def group(g, k):
                        if there(g + 1):
                            load(g + 1, 1 - k)
                        sp.wait_ge(y_ready, G * (g + 1))
                        sp.dma_start(out_groups[g, :, :, :], out_sb[k][:]).then_inc(out_stored[k], 16)

                    load(0, 0)
                    groups(sp, group)
                    for k in range(2):
                        sp.wait_ge(out_stored[k], 8 * NG)

                @block.tensor
                def _(pe):
                    def turn_tokens(g):
                        pe.wait_ge(n2_ready, g + 1)
                        for c in range(C):
                            if c < 2:
                                if not isinstance(g, int) or g > 0:
                                    pe.wait_ge(n2Tlo_ready, C * g if c == 0 else C * (g - 1) + 2)
                            else:
                                pe.wait_ge(n2Tlo_ready, C * g + 1)
                            for t in range(G):
                                last = pe.transpose(n2T_bank[c][:, t * P:(t + 1) * P],
                                                    n2[:, t, c * P:(c + 1) * P], ident[:])
                            last.then_inc(n2T_done, 1)

                    def route(g):
                        if not isinstance(g, int) or g > 0:
                            pe.wait_ge(oneT_ready, g)
                        for c in range(C):
                            pe.wait_ge(n2Thi_ready, C * g + c + 1)
                            pe.matmul(logitsT_bank[:, :], route_w[:, c, :], n2T_hi[:, c, :],
                                      start=(c == 0), stop=False)
                        for c in range(C):
                            pe.wait_ge(n2Tlo_ready, C * g + c + 1)
                            last = pe.matmul(logitsT_bank[:, :], route_w[:, c, :], n2T_lo[:, c, :],
                                             start=False, stop=(c == C - 1))
                        last.then_inc(logitsT_done, 1)

                    def turn_logits(g):
                        pe.wait_ge(logitsT_ready, g + 1)
                        if not isinstance(g, int) or g > 0:
                            pe.wait_ge(parts_ready, g)
                        pe.nop(nofuse=True)
                        for t in range(G):
                            last = pe.transpose(small_bank[:, t * ROUTE:(t + 1) * ROUTE],
                                                logitsT[:, t * P:(t + 1) * P], ident[0:ROUTE, 0:ROUTE])
                        last.then_inc(parts_done, 1)

                    def turn_one_hot(g):
                        pe.wait_ge(one_hot_ready, g + 1)
                        pe.nop(nofuse=True)
                        for t in range(G):
                            last = pe.transpose(logitsT_bank[0:ROUTE, t * P:(t + 1) * P].bitcast(F32R),
                                                one_hot[:, t, :], ident_r[:])
                        last.then_inc(oneT_done, 1)

                    def hidden(g, k):
                        for q in range(Q):
                            if q >= 2:
                                pe.wait_ge(gelu_ready, Q * g + q - 1)
                            elif not isinstance(g, int) or g > 0:
                                pe.wait_ge(gelu_ready, Q * (g - 1) + q + 3)
                            o = hidden_bank[q % 2][:, :]
                            for c in range(C):
                                w_hi, w_lo = (w[:, c, q * P:(q + 1) * P] for w in (w1_hi, w1_lo))
                                pe.matmul(o, w_hi, n2T_hi[:, c, :], start=(c == 0), stop=False)
                                pe.matmul(o, w_hi, n2T_lo[:, c, :], start=False, stop=False)
                                pe.matmul(o, w_lo, n2T_hi[:, c, :], start=False, stop=False)
                            pe.wait_ge(oneT_ready, g + 1)
                            pe.matmul(o, switch_off[:, q, :], oneT[k][:], start=False, stop=True
                                      ).then_inc(hidden_done, 1)

                    def output(g, k, t):
                        if t >= 2:
                            pe.wait_ge(y_ready, G * g + t - 1)
                        elif not isinstance(g, int) or g > 0:
                            pe.wait_ge(y_ready, G * (g - 1) + t + 3)
                        o = y_bank[t % 2][:, 0:D]
                        tok = slice(t * P, (t + 1) * P)
                        for q in range(Q):
                            if t == 0:
                                pe.wait_ge(geluhi_ready, Q * g + q + 1)
                                pe.wait_ge(gelulo_ready, Q * g + q + 1)
                            pe.matmul(o, gelu_hi[:, q, tok], w2_hi[:, q, :], start=(q == 0), stop=False)
                            pe.matmul(o, gelu_hi[:, q, tok], w2_lo[:, q, :], start=False, stop=False)
                            pe.matmul(o, gelu_lo[:, q, tok], w2_hi[:, q, :], start=False, stop=False)
                        pe.matmul(o, oneT[k][:, tok], b2_rows[:], start=False, stop=True).then_inc(y_done, 1)

                    def group(g, k):
                        hidden(g, k)
                        if there(g + 1):
                            turn_tokens(g + 1)
                            route(g + 1)
                        output(g, k, 0)
                        if there(g + 1):
                            turn_logits(g + 1)
                        output(g, k, 1)
                        output(g, k, 2)
                        if there(g + 1):
                            turn_one_hot(g + 1)
                        output(g, k, 3)

                    turn_tokens(0)
                    route(0)
                    turn_logits(0)
                    turn_one_hot(0)
                    groups(pe, group)

                @block.scalar
                def _(act):
                    def normalise(g, k):
                        act.wait_ge(shift2_done, g + 1)
                        if not isinstance(g, int) or g > 0:
                            act.wait_ge(n2T_done, C * g)
                        for t in range(G):
                            last = act.activation(n2[:, t, :], x1[k][:, t, :], ACT.Identity,
                                                  bias=shift2[:, t:t + 1], scale=scale2[:, t:t + 1])
                        last.then_inc(n2_ready, 1)

                    def copy_tokensT(g):
                        if not isinstance(g, int) or g > 0:
                            act.wait_ge(hidden_done, Q * g)
                        for c in range(C):
                            act.wait_ge(n2T_done, C * g + c + 1)
                            act.copy(n2T_hi[:, c, :], n2T_bank[c][:, :]).then_inc(n2Thi_ready, 1)

                    def copy_logitsT(g):
                        act.wait_ge(logitsT_done, g + 1)
                        act.copy(logitsT[:], logitsT_bank[0:ROUTE, :]).then_inc(logitsT_ready, 1)

                    def copy_one_hotT(g, k):
                        act.wait_ge(oneT_done, g + 1)
                        if not isinstance(g, int) or g > 1:
                            act.wait_ge(y_done, G * (g - 1))
                        act.copy(oneT[k][:], logitsT_bank[0:ROUTE, :]).then_inc(oneT_ready, 1)

                    def gelu(g, q):
                        act.wait_ge(hidden_done, Q * g + q + 1)
                        if not isinstance(g, int) or g > 0:
                            act.wait_ge(gelulo_ready, Q * (g - 1) + q + 1)
                        act.activation(gelu_out[:, q, :], hidden_bank[q % 2][:, :], ACT.Gelu,
                                       bias=b1_col[:, q:q + 1]).then_inc(gelu_ready, 1)

                    def group(g, k):
                        gelu(g, 0)
                        gelu(g, 1)
                        if there(g + 1):
                            normalise(g + 1, 1 - k)
                        gelu(g, 2)
                        gelu(g, 3)
                        if there(g + 1):
                            copy_tokensT(g + 1)
                            copy_logitsT(g + 1)
                            copy_one_hotT(g + 1, 1 - k)

                    assert Q == 4
                    normalise(0, 0)
                    copy_tokensT(0)
                    copy_logitsT(0)
                    copy_one_hotT(0, 0)
                    groups(act, group)

                @block.vector
                def _(dve):
                    def stats(g, k):
                        dve.wait_ge(x1_loaded[k], 8 * (g - k) + 16)
                        for t in range(G):
                            last = dve.bn_stats(bn2[:, t, :], x1[k][:, t, :])
                        last.then_inc(bn2_done, 1)
                        dve.wait_ge(bn2_done, g + 1)
                        if not isinstance(g, int) or g > 0:
                            dve.wait_ge(shift2_done, g)
                        dve.nop(nofuse=True)
                        for t in range(G):
                            last = dve.bn_aggr(mv2[:, t, :], bn2[:, t, :])
                        last.then_inc(mv2_done, 1)

                    def gelu_high(g, q):
                        dve.wait_ge(gelu_ready, Q * g + q + 1)
                        if not isinstance(g, int) or g > 0:
                            dve.wait_ge(y_done, G * g)
                        dve.tensor_copy(gelu_hi[:, q, :], gelu_out[:, q, :]).then_inc(geluhi_ready, 1)

                    def tokensT_low(g):
                        for c in range(C):
                            dve.wait_ge(n2Thi_ready, C * g + c + 1)
                            dve.tensor_tensor(n2T_lo[:, c, :], n2T_bank[c][:, :], n2T_hi[:, c, :].bitcast(F32),
                                              ALU.subtract).then_inc(n2Tlo_ready, 1)

                    def route_first(g):
                        dve.wait_ge(parts_done, g + 1)
                        dve.tensor_copy(parts[:], small_bank[:, 0:G * ROUTE].rearrange("p (t r) -> p t r", t=G)
                                        ).then_inc(parts_ready, 1)
                        dve.wait_ge(parts_ready, g + 1)
                        dve.tensor_tensor(raw[:], parts[:, :, 0:E], parts[:, :, SPLIT:ROUTE], ALU.add
                                          ).then_inc(raw_done, 1)
                        dve.wait_ge(raw_done, g + 1)
                        dve.tensor_tensor(logits[:], raw[:], route_b[:].unsqueeze(1).broadcast_to([P, G, E]),
                                          ALU.add).then_inc(logits_done, 1)
                        dve.wait_ge(logits_done, g + 1)
                        dve.tensor_reduce(top[:], logits[:], AX_X, ALU.max).then_inc(top_done, 1)
                        dve.wait_ge(top_done, g + 1)
                        if not isinstance(g, int) or g > 0:
                            dve.wait_ge(odds_ready, g)
                        dve.tensor_tensor(below_top[:], logits[:], top[:].unsqueeze(2).broadcast_to([P, G, E]),
                                          ALU.subtract).then_inc(below_done, 1)
                        dve.tensor_tensor(is_top[:], logits[:], top[:].unsqueeze(2).broadcast_to([P, G, E]),
                                          ALU.is_equal).then_inc(is_top_done, 1)

                    def route_second(g):
                        dve.wait_ge(is_top_done, g + 1)
                        dve.wait_ge(consts_made, 1)
                        dve.tensor_tensor(key[:], is_top[:], rank[:], ALU.mult).then_inc(key_done, 1)
                        dve.wait_ge(key_done, g + 1)
                        dve.tensor_reduce(best[:], key[:], AX_X, ALU.max).then_inc(best_done, 1)
                        dve.wait_ge(best_done, g + 1)
                        if not isinstance(g, int) or g > 0:
                            dve.wait_ge(oneT_done, g)
                        for col in (0, SPLIT):
                            last = dve.tensor_tensor(one_hot[:, :, col:col + E], key[:],
                                                     best[:].unsqueeze(2).broadcast_to([P, G, E]), ALU.is_equal)
                        last.then_inc(one_hot_ready, 1)

                    def probability(g, k):
                        dve.wait_ge(odds_ready, g + 1)
                        dve.tensor_reduce(odds_sum[:], odds[:], AX_X, ALU.add).then_inc(odds_sum_done, 1)
                        dve.wait_ge(odds_sum_done, g + 1)
                        dve.reciprocal(top_prob[k][:], odds_sum[:]).then_inc(prob_ready, 1)

                    def combine(g, k, t):
                        dve.wait_ge(y_done, G * g + t + 1)
                        if t == 0:
                            dve.wait_ge(prob_ready, g + 1)
                            if not isinstance(g, int) or g > 1:
                                dve.wait_ge(out_stored[k], 8 * (g - k))
                        dve.scalar_tensor_tensor(out_sb[k][:, t, :], y_bank[t % 2][:, 0:D], top_prob[k][:, t:t + 1],
                                                 x1[k][:, t, :], ALU.mult, ALU.add).then_inc(y_ready, 1)

                    def group(g, k):
                        if there(g + 1):
                            stats(g + 1, 1 - k)
                        for q in range(Q):
                            gelu_high(g, q)
                        if there(g + 1):
                            tokensT_low(g + 1)
                        combine(g, k, 0)
                        if there(g + 1):
                            route_first(g + 1)
                            route_second(g + 1)
                        combine(g, k, 1)
                        if there(g + 1):
                            probability(g + 1, 1 - k)
                        combine(g, k, 2)
                        combine(g, k, 3)

                    dve.memset(one_hot[:].bitcast(F32), 0.0)
                    stats(0, 0)
                    tokensT_low(0)
                    route_first(0)
                    route_second(0)
                    probability(0, 0)
                    groups(dve, group)

                @block.gpsimd
                def _(pool):
                    def token_scale(g):
                        pool.wait_ge(mv2_done, g + 1)
                        if not isinstance(g, int) or g > 0:
                            pool.wait_ge(n2_ready, g)
                        pool.nop(nofuse=True)
                        pool.tensor_scalar(var2[:], mv2[:, :, 1], LN_INPUT_EPS, None, ALU.add).then_inc(var2_done, 1)
                        pool.wait_ge(var2_done, g + 1)
                        pool.tensor_tensor(scale2[:], var2[:], minus_half[:], ALU.pow).then_inc(scale2_done, 1)
                        pool.wait_ge(scale2_done, g + 1)
                        pool.tensor_tensor(shift2a[:], mv2[:, :, 0], scale2[:], ALU.mult).then_inc(shift2a_done, 1)
                        pool.wait_ge(shift2a_done, g + 1)
                        pool.nop(nofuse=True)
                        pool.tensor_scalar(shift2[:], shift2a[:], -1.0, None, ALU.mult).then_inc(shift2_done, 1)

                    def gelu_low(g, q):
                        pool.wait_ge(geluhi_ready, Q * g + q + 1)
                        pool.tensor_tensor(gelu_lo[:, q, :], gelu_out[:, q, :], gelu_hi[:, q, :].bitcast(F32),
                                           ALU.subtract).then_inc(gelulo_ready, 1)

                    def exponentials(g):
                        pool.wait_ge(below_done, g + 1)
                        if not isinstance(g, int) or g > 0:
                            pool.wait_ge(odds_sum_done, g)
                        pool.tensor_tensor(odds[:], euler[:], below_top[:], ALU.pow).then_inc(odds_ready, 1)

                    def group(g, k):
                        gelu_low(g, 0)
                        if there(g + 1):
                            token_scale(g + 1)
                        for q in range(1, Q):
                            gelu_low(g, q)
                        if there(g + 1):
                            exponentials(g + 1)

                    pool.memset(euler[:], float(np.e))
                    for e in range(E):
                        last = pool.memset(rank[:, :, e:e + 1], float(E - e))
                    last.then_inc(consts_made, 1)
                    token_scale(0)
                    exponentials(0)
                    groups(pool, group)


_INS = ["x", "adj", "L0_gnn_Wl", "L0_gnn_bl", "L0_gnn_Ws", "L0_gnn_bs", "L0_gnn_Wr", "L0_gnn_br",
        "L0_gnn_ln_w", "L0_gnn_ln_b", "L0_ffn_enc_w", "L0_ffn_enc_b", "L0_ffn_sw_w", "L0_ffn_sw_b",
        "L0_ffn_w1", "L0_ffn_b1", "L0_ffn_w2", "L0_ffn_b2"]
_OUTS = [((128, 128, 384), "float32")]


def kernel(**inputs):
    import numpy as _np
    import concourse.bacc as _bacc
    from concourse import mybir as _mybir
    from concourse.bass_utils import run_bass_kernel_spmd as _run

    nc = _bacc.Bacc("TRN2", target_bir_lowering=False, num_devices=1)
    arrays, args = {}, []
    for name in _INS:
        a = _np.ascontiguousarray(inputs[name])
        arrays[f"in_{name}_dram"] = a
        args.append(nc.dram_tensor(f"in_{name}_dram", a.shape, _mybir.dt.from_np(a.dtype), kind="ExternalInput").ap())
    for i, (shape, dtype) in enumerate(_OUTS):
        dt = _mybir.dt.from_np(_np.dtype(dtype))
        args.append(nc.dram_tensor(f"out_{i}_dram", shape, dt, kind="ExternalOutput").ap())
    build(nc, *args)
    r = _run(nc, [arrays], core_ids=[0])
    got = tuple(r.results[0][f"out_{i}_dram"] for i in range(len(_OUTS)))
    return got[0]
```

```python
from contextlib import ExitStack

import numpy as np

import concourse.bass as bass
from concourse import mybir

F32 = mybir.dt.float32
F32R = mybir.dt.float32r
ALU = mybir.AluOpType
ACT = mybir.ActivationFunctionType
AX_X = mybir.AxisListType.X

P = 128
LN_INPUT_EPS = 1e-5
LN_LAYER_EPS = 1e-12
DENOM_EPS = 1e-10
SWITCHED_OFF = float(2 ** 40)
SPLIT = 32


def build(nc, x, adj, Wl, bl, Ws, bs, Wr, br, ln_w, ln_b,
          enc_w, enc_b, sw_w, sw_b, w1, b1, w2, b2, out):
    B, S, D = x.shape
    L = Wl.shape[0]
    C = D // P
    E, _, R = w1.shape
    Q = E * R // P
    G = 4
    NG = B // G
    TOK = G * P
    assert S == P and D == C * P and L == 2 and E * R == Q * P and TOK == 512 and NG % 4 == 0 and B >= 8

    ctx = ExitStack()
    with ctx:
        def sb(name, shape, dt=F32, where=ctx):
            return where.enter_context(nc.sbuf_tensor(name, shape, dt))

        def sem(name):
            return ctx.enter_context(nc.semaphore(name))

        def per_layer(name):
            return [sem(f"{name}{l}") for l in range(L)]

        x1_dram = nc.dram_tensor("x1_scratch", [B, S, D], F32, kind="Internal").ap()
        bank = [ctx.enter_context(nc.psum_tensor(f"bank{k}", [P, 512], F32)) for k in range(8)]

        ident = sb("ident", [P, P])
        ident_r = sb("ident_r", [P, P], F32R)
        minus_half = sb("minus_half", [P, G])
        w1_hi = sb("w1_hi", [P, C, E * R], F32R)
        w1_lo = sb("w1_lo", [P, C, E * R], F32R)
        w2_hi = sb("w2_hi", [P, Q, D], F32R)
        w2_lo = sb("w2_lo", [P, Q, D], F32R)
        b1_col = sb("b1_col", [P, Q])
        route_w = sb("route_w", [P, C, P], F32R)
        route_b = sb("route_b", [P, E])
        b2_rows = sb("b2_rows", [SPLIT + E, D], F32R)
        switch_off = sb("switch_off", [SPLIT + E, Q, P], F32R)

        BK = 2 * SPLIT + 3
        enc_in = sb("enc_in", [P, C, R])
        encT = sb("encT", [R, C, P])
        sw_in = sb("sw_in", [R, E])
        encb_col = sb("encb_col", [R, 1])
        encb_wide = sb("encb_wide", [R, P])
        swb_all = sb("swb_all", [P, E])
        ones = sb("ones", [R, P])

        ROUTE = SPLIT + E
        RING = 4
        with ExitStack() as setup_ctx:
            stage = sb("stage", [P, 3, L, C, D], F32, setup_ctx)
            bias_in = sb("bias_in", [BK, L, D], F32, setup_ctx)
            b2_in = sb("b2_in", [SPLIT + E, D], F32, setup_ctx)
        x1 = [sb(f"x1_{r}", [P, G, D]) for r in range(2)]
        n2 = sb("n2", [P, G, D])
        n2T_hi, n2T_lo = ([sb(f"{name}0", [P, C, TOK], F32R)] for name in ("n2T_hi", "n2T_lo"))
        oneT = [sb("oneT0", [ROUTE, TOK], F32R)]
        assert D * Q == G * D and C * E * R == G * D
        w1_in = x1[0][:].rearrange("p t d -> p (t d)").rearrange("p (c k) -> p c k", c=C)
        w2_in = x1[1][:].rearrange("p t d -> p (t d)").rearrange("p (q d) -> p q d", q=Q)
        w_pieces = ([(w1_hi[:, c, :], w1_lo[:, c, :], w1_in[:, c, :]) for c in range(C)] +
                    [(w2_hi[:, q, :], w2_lo[:, q, :], w2_in[:, q, :]) for q in range(Q)])

        def pieces(i, half):
            k = 2 * (i - 1) + half if isinstance(i, int) and i > 0 else len(w_pieces)
            return range(2 * k, min(2 * k + 2, len(w_pieces)))

        top_prob = [sb(f"top_prob{k}", [P, G]) for k in range(2)]
        bn2 = sb("bn2", [P, G, 6])
        mv2 = sb("mv2", [P, G, 2])
        var2 = sb("var2", [P, G])
        scale2 = sb("scale2", [P, G])
        shift2a = sb("shift2a", [P, G])
        shift2 = sb("shift2", [P, G])
        euler = sb("euler", [P, G, E])
        rank = sb("rank", [P, G, E])
        logitsT = sb("logitsT", [ROUTE, TOK])
        parts = sb("parts", [P, G, ROUTE])
        raw = sb("raw", [P, G, E])
        logits = sb("logits", [P, G, E])
        top = sb("top", [P, G])
        is_top = sb("is_top", [P, G, E])
        key = sb("key", [P, G, E])
        best = sb("best", [P, G])
        one_hot = sb("one_hot", [P, G, ROUTE], F32R)
        below_top = sb("below_top", [P, G, E])
        odds = sb("odds", [P, G, E])
        odds_sum = sb("odds_sum", [P, G])


        const_in, ffn_in = sem("const_in"), sem("ffn_in")
        wt_in = [sem(f"wt_in{l}") for l in range(L)]
        bias_in_loaded = sem("bias_in_loaded")
        bias_zeroed, bias_made, b2_high_made = sem("bias_zeroed"), sem("bias_made"), sem("b2_high_made")
        bias_high_made, w_high_made, w_low_made = sem("bias_high_made"), sem("w_high_made"), sem("w_low_made")
        zeroed, ident_made, ident_r_made = sem("zeroed"), sem("ident_made"), sem("ident_r_made")
        filled = sem("filled")
        wT_done, wT_hi_made, wT_lo_made = sem("wT_done"), sem("wT_hi_made"), sem("wT_lo_made")
        encT_done, encT_made, encb_made = sem("encT_done"), sem("encT_made"), sem("encb_made")
        route_done, route_hi_made, route_made = sem("route_done"), sem("route_hi_made"), sem("route_made")

        names = ("bn2_done mv2_done var2_done scale2_done shift2a_done shift2_done n2_act_ready n2_dve_ready "
                 "consts_made logitsT_done logitsT_ready parts_done parts_ready raw_done "
                 "logits_done top_done below_done odds_ready odds_sum_done prob_ready is_top_done "
                 "key_done best_done one_hot_ready oneT_done oneT_ready").split()
        (bn2_done, mv2_done, var2_done, scale2_done, shift2a_done, shift2_done, n2_act_ready,
         n2_dve_ready,
         consts_made, logitsT_done, logitsT_ready, parts_done, parts_ready, raw_done,
         logits_done, top_done, below_done, odds_ready, odds_sum_done, prob_ready, is_top_done,
         key_done, best_done, one_hot_ready, oneT_done, oneT_ready) = map(sem, names)
        x1_loaded = [sem(f"x1_loaded_{r}") for r in range(RING)]
        out_stored = [sem(f"out_stored_{k}") for k in range(2)]
        n2T_done, n2Thi_ready, n2Tlo_ready = map(sem, ("n2T_done", "n2Thi_ready", "n2Tlo_ready"))
        hidden_done, gelu_ready, geluhi_ready = map(sem, ("hidden_done", "gelu_ready", "geluhi_ready"))
        gelulo_ready, gelulast_ready = map(sem, ("gelulo_ready", "gelulast_ready"))
        y_done, y_ready = map(sem, ("y_done", "y_ready"))

        n2T_bank = (bank[5], bank[6], bank[7])
        logitsT_bank, small_bank = bank[2], bank[7]
        hidden_bank = (bank[3], bank[4])
        y_bank = (bank[0], bank[1])

        x1_groups = x1_dram.rearrange("(g t) p d -> g p t d", t=G)
        out_groups = out.rearrange("(g t) p d -> g p t d", t=G)

        def there(g):
            return not isinstance(g, int) or g < NG

        def ffn_tensor(pe):
            def turn_tokens(g, c):
                if c == 0:
                    pe.wait_ge(n2_act_ready, g + 1)
                    pe.wait_ge(n2_dve_ready, g + 1)
                if isinstance(g, int) and g == 0:
                    pe.wait_ge(agglo_ready[L - 1], C * (B - 1) + c + 1)
                else:
                    if c < 2:
                        pe.wait_ge(n2Tlo_ready, C * (g - 1) + c + 1)
                    else:
                        pe.wait_ge(parts_ready, g)
                for t in range(G):
                    last = pe.transpose(n2T_bank[c][:, t * P:(t + 1) * P],
                                        n2[:, t, c * P:(c + 1) * P], ident[:])
                last.then_inc(n2T_done, 1)

            def route(g, j):
                if isinstance(g, int) and g == 0:
                    pe.wait_ge(deltaTlo_ready[L - 1], B)
                    pe.wait_ge(route_made, 1)
                else:
                    pe.wait_ge(oneT_ready, g)
                for c in range(C):
                    pe.wait_ge(n2Thi_ready, C * g + c + 1)
                    pe.matmul(logitsT_bank[:, :], route_w[:, c, :], n2T_hi[j][:, c, :],
                              start=(c == 0), stop=False)
                for c in range(C):
                    pe.wait_ge(n2Tlo_ready, C * g + c + 1)
                    last = pe.matmul(logitsT_bank[:, :], route_w[:, c, :], n2T_lo[j][:, c, :],
                                     start=False, stop=(c == C - 1))
                last.then_inc(logitsT_done, 1)

            def turn_logits(g):
                pe.wait_ge(logitsT_ready, g + 1)
                if not isinstance(g, int) or g > 0:
                    pe.wait_ge(parts_ready, g)
                pe.nop(nofuse=True)
                for t in range(G):
                    last = pe.transpose(small_bank[:, t * ROUTE:(t + 1) * ROUTE],
                                        logitsT[:, t * P:(t + 1) * P], ident[0:ROUTE, 0:ROUTE])
                last.then_inc(parts_done, 1)

            def turn_one_hot(g):
                pe.wait_ge(one_hot_ready, g + 1)
                pe.nop(nofuse=True)
                for t in range(G):
                    last = pe.transpose(logitsT_bank[0:ROUTE, t * P:(t + 1) * P].bitcast(F32R),
                                        one_hot[:, t, :], ident_r[:])
                last.then_inc(oneT_done, 1)

            def hidden(g, j, q):
                if q >= 2:
                    pe.wait_ge(gelu_ready, Q * g + q - 1)
                elif not isinstance(g, int) or g > 0:
                    pe.wait_ge(gelu_ready, Q * (g - 1) + q + 3)
                o = hidden_bank[q % 2][:, :]
                for c in range(C):
                    w_hi, w_lo = (w[:, c, q * P:(q + 1) * P] for w in (w1_hi, w1_lo))
                    pe.matmul(o, w_hi, n2T_hi[j][:, c, :], start=(c == 0), stop=False)
                    pe.matmul(o, w_hi, n2T_lo[j][:, c, :], start=False, stop=False)
                    pe.matmul(o, w_lo, n2T_hi[j][:, c, :], start=False, stop=False)
                pe.wait_ge(oneT_ready, g + 1)
                pe.matmul(o, switch_off[:, q, :], oneT[j][:], start=False, stop=True
                          ).then_inc(hidden_done, 1)

            def output(g, k, t):
                if t >= 2:
                    pe.wait_ge(y_ready, G * g + t - 1)
                elif not isinstance(g, int) or g > 0:
                    pe.wait_ge(y_ready, G * (g - 1) + t + 3)
                o = y_bank[t % 2][:, 0:D]
                tok = slice(t * P, (t + 1) * P)
                for q in range(Q):
                    if t == 0:
                        if q < Q - 1:
                            pe.wait_ge(gelulo_ready, (Q - 1) * g + q + 1)
                        else:
                            pe.wait_ge(gelulast_ready, g + 1)
                    pe.matmul(o, gelu_hi[:, q, tok], w2_hi[:, q, :], start=(q == 0), stop=False)
                    pe.matmul(o, gelu_hi[:, q, tok], w2_lo[:, q, :], start=False, stop=False)
                    pe.matmul(o, gelu_lo[:, q, tok], w2_hi[:, q, :], start=False, stop=False)
                pe.matmul(o, oneT[k][:, tok], b2_rows[:], start=False, stop=True).then_inc(y_done, 1)

            def group(g, r):
                j, following = r % 2, there(g + 1)
                for q in range(Q - 1):
                    hidden(g, j, q)
                if following:
                    for c in range(C):
                        turn_tokens(g + 1, c)
                hidden(g, j, Q - 1)
                if following:
                    route(g + 1, 1 - j)
                output(g, j, 0)
                if following:
                    turn_logits(g + 1)
                output(g, j, 1)
                output(g, j, 2)
                if following:
                    turn_one_hot(g + 1)
                output(g, j, 3)

            return turn_tokens, route, turn_logits, turn_one_hot, group

        def ffn_scalar(act):
            def normalise(g, r):
                act.wait_ge(shift2_done, g + 1)
                if not isinstance(g, int) or g > 0:
                    act.wait_ge(n2T_done, C * g)
                for t in range(G // 2, G):
                    last = act.activation(n2[:, t, :], x1[r][:, t, :], ACT.Identity,
                                          bias=shift2[:, t:t + 1], scale=scale2[:, t:t + 1])
                last.then_inc(n2_act_ready, 1)

            def copy_tokensT(g, j, c):
                act.wait_ge(n2T_done, C * g + c + 1)
                if not isinstance(g, int) or g > 1:
                    act.wait_ge(hidden_done, Q * (g - 1))
                act.copy(n2T_hi[j][:, c, :], n2T_bank[c][:, :]).then_inc(n2Thi_ready, 1)

            def copy_logitsT(g):
                act.wait_ge(logitsT_done, g + 1)
                act.copy(logitsT[:], logitsT_bank[0:ROUTE, :]).then_inc(logitsT_ready, 1)

            def copy_one_hotT(g, k):
                act.wait_ge(oneT_done, g + 1)
                if not isinstance(g, int) or g > 1:
                    act.wait_ge(y_done, G * (g - 1))
                act.copy(oneT[k][:], logitsT_bank[0:ROUTE, :]).then_inc(oneT_ready, 1)

            def gelu(g, q):
                act.wait_ge(hidden_done, Q * g + q + 1)
                if not isinstance(g, int) or g > 0:
                    if q < Q - 1:
                        act.wait_ge(gelulo_ready, (Q - 1) * (g - 1) + q + 1)
                    else:
                        act.wait_ge(gelulast_ready, g)
                act.activation(gelu_out[:, q, :], hidden_bank[q % 2][:, :], ACT.Gelu,
                               bias=b1_col[:, q:q + 1]).then_inc(gelu_ready, 1)

            def group(g, r):
                j, following = r % 2, there(g + 1)
                gelu(g, 0)
                if following:
                    normalise(g + 1, (r + 1) % RING)
                gelu(g, 1)
                gelu(g, 2)
                if following:
                    for c in range(C):
                        copy_tokensT(g + 1, 1 - j, c)
                gelu(g, 3)
                if following:
                    copy_logitsT(g + 1)
                    copy_one_hotT(g + 1, 1 - j)

            return normalise, copy_tokensT, copy_logitsT, copy_one_hotT, group

        def ffn_vector(dve):
            def stats(g, r):
                dve.wait_ge(x1_loaded[r], 16 // RING * (g - r) + 16)
                for t in range(G):
                    last = dve.bn_stats(bn2[:, t, :], x1[r][:, t, :])
                last.then_inc(bn2_done, 1)
                dve.wait_ge(bn2_done, g + 1)
                if not isinstance(g, int) or g > 0:
                    dve.wait_ge(shift2_done, g)
                dve.nop(nofuse=True)
                for t in range(G):
                    last = dve.bn_aggr(mv2[:, t, :], bn2[:, t, :])
                last.then_inc(mv2_done, 1)

            def gelu_high(g, q):
                dve.wait_ge(gelu_ready, Q * g + q + 1)
                if not isinstance(g, int) or g > 0:
                    dve.wait_ge(y_done, G * g)
                dve.tensor_copy(gelu_hi[:, q, :], gelu_out[:, q, :]).then_inc(geluhi_ready, 1)

            def normalise(g, r):
                dve.wait_ge(shift2_done, g + 1)
                if not isinstance(g, int) or g > 0:
                    dve.wait_ge(n2T_done, C * g)
                for t in range(G // 2):
                    last = dve.tensor_scalar(n2[:, t, :], x1[r][:, t, :], scale2[:, t:t + 1],
                                             shift2[:, t:t + 1], ALU.mult, ALU.add)
                last.then_inc(n2_dve_ready, 1)

            def gelu_low(g, q):
                dve.wait_ge(geluhi_ready, Q * g + q + 1)
                dve.tensor_tensor(gelu_lo[:, q, :], gelu_out[:, q, :], gelu_hi[:, q, :].bitcast(F32),
                                  ALU.subtract).then_inc(gelulast_ready, 1)

            def tokensT_low(g, j, c):
                dve.wait_ge(n2Thi_ready, C * g + c + 1)
                dve.tensor_tensor(n2T_lo[j][:, c, :], n2T_bank[c][:, :], n2T_hi[j][:, c, :].bitcast(F32),
                                  ALU.subtract).then_inc(n2Tlo_ready, 1)

            def route_first(g):
                dve.wait_ge(parts_done, g + 1)
                dve.tensor_copy(parts[:], small_bank[:, 0:G * ROUTE].rearrange("p (t r) -> p t r", t=G)
                                ).then_inc(parts_ready, 1)
                dve.wait_ge(parts_ready, g + 1)
                dve.tensor_tensor(raw[:], parts[:, :, 0:E], parts[:, :, SPLIT:ROUTE], ALU.add
                                  ).then_inc(raw_done, 1)
                dve.wait_ge(raw_done, g + 1)
                dve.tensor_tensor(logits[:], raw[:], route_b[:].unsqueeze(1).broadcast_to([P, G, E]),
                                  ALU.add).then_inc(logits_done, 1)
                dve.wait_ge(logits_done, g + 1)
                dve.tensor_reduce(top[:], logits[:], AX_X, ALU.max).then_inc(top_done, 1)
                dve.wait_ge(top_done, g + 1)
                if not isinstance(g, int) or g > 0:
                    dve.wait_ge(odds_ready, g)
                dve.tensor_tensor(below_top[:], logits[:], top[:].unsqueeze(2).broadcast_to([P, G, E]),
                                  ALU.subtract).then_inc(below_done, 1)
                dve.tensor_tensor(is_top[:], logits[:], top[:].unsqueeze(2).broadcast_to([P, G, E]),
                                  ALU.is_equal).then_inc(is_top_done, 1)

            def route_second(g):
                dve.wait_ge(is_top_done, g + 1)
                dve.wait_ge(consts_made, 1)
                dve.tensor_tensor(key[:], is_top[:], rank[:], ALU.mult).then_inc(key_done, 1)
                dve.wait_ge(key_done, g + 1)
                dve.tensor_reduce(best[:], key[:], AX_X, ALU.max).then_inc(best_done, 1)
                dve.wait_ge(best_done, g + 1)
                if not isinstance(g, int) or g > 0:
                    dve.wait_ge(oneT_done, g)
                for col in (0, SPLIT):
                    last = dve.tensor_tensor(one_hot[:, :, col:col + E], key[:],
                                             best[:].unsqueeze(2).broadcast_to([P, G, E]), ALU.is_equal)
                last.then_inc(one_hot_ready, 1)

            def probability(g, k):
                dve.wait_ge(odds_ready, g + 1)
                dve.tensor_reduce(odds_sum[:], odds[:], AX_X, ALU.add).then_inc(odds_sum_done, 1)
                dve.wait_ge(odds_sum_done, g + 1)
                dve.reciprocal(top_prob[k][:], odds_sum[:]).then_inc(prob_ready, 1)

            def combine(g, r, t):
                k = r % 2
                dve.wait_ge(y_done, G * g + t + 1)
                if t == 0:
                    dve.wait_ge(prob_ready, g + 1)
                    if not isinstance(g, int) or g > 1:
                        dve.wait_ge(out_stored[k], 8 * (g - k))
                dve.scalar_tensor_tensor(out_sb[k][:, t, :], y_bank[t % 2][:, 0:D], top_prob[k][:, t:t + 1],
                                         x1[r][:, t, :], ALU.mult, ALU.add).then_inc(y_ready, 1)

            def group(g, r):
                j, following = r % 2, there(g + 1)
                if following:
                    normalise(g + 1, (r + 1) % RING)
                gelu_high(g, 0)
                gelu_high(g, 1)
                gelu_high(g, 2)
                if following:
                    for c in range(C):
                        tokensT_low(g + 1, 1 - j, c)
                probability(g, j)
                gelu_high(g, 3)
                gelu_low(g, 3)
                combine(g, r, 0)
                if following:
                    route_first(g + 1)
                    route_second(g + 1)
                combine(g, r, 1)
                if there(g + 2):
                    stats(g + 2, (r + 2) % RING)
                combine(g, r, 2)
                combine(g, r, 3)

            return stats, normalise, tokensT_low, route_first, route_second, group

        def ffn_gpsimd(pool):
            def token_scale(g):
                pool.wait_ge(mv2_done, g + 1)
                if not isinstance(g, int) or g > 0:
                    pool.wait_ge(n2_act_ready, g)
                    pool.wait_ge(n2_dve_ready, g)
                pool.nop(nofuse=True)
                pool.tensor_scalar(var2[:], mv2[:, :, 1], LN_INPUT_EPS, None, ALU.add).then_inc(var2_done, 1)
                pool.wait_ge(var2_done, g + 1)
                pool.tensor_tensor(scale2[:], var2[:], minus_half[:], ALU.pow).then_inc(scale2_done, 1)
                pool.wait_ge(scale2_done, g + 1)
                pool.tensor_tensor(shift2a[:], mv2[:, :, 0], scale2[:], ALU.mult).then_inc(shift2a_done, 1)
                pool.wait_ge(shift2a_done, g + 1)
                pool.nop(nofuse=True)
                pool.tensor_scalar(shift2[:], shift2a[:], -1.0, None, ALU.mult).then_inc(shift2_done, 1)

            def gelu_low(g, q):
                pool.wait_ge(geluhi_ready, Q * g + q + 1)
                pool.tensor_tensor(gelu_lo[:, q, :], gelu_out[:, q, :], gelu_hi[:, q, :].bitcast(F32),
                                   ALU.subtract).then_inc(gelulo_ready, 1)

            def exponentials(g):
                pool.wait_ge(below_done, g + 1)
                if not isinstance(g, int) or g > 0:
                    pool.wait_ge(odds_sum_done, g)
                pool.tensor_tensor(odds[:], euler[:], below_top[:], ALU.pow).then_inc(odds_ready, 1)

            def group(g, r):
                if there(g + 1):
                    token_scale(g + 1)
                for q in range(Q - 1):
                    gelu_low(g, q)
                if there(g + 1):
                    exponentials(g + 1)

            return token_scale, exponentials, group

        gnn_ctx = ExitStack()
        with gnn_ctx:
            wT_hi = sb("wT_hi", [P, L, 3, C, D], F32R, gnn_ctx)
            wT_lo = sb("wT_lo", [P, L, 3, C, D], F32R, gnn_ctx)
            bias_rows = sb("bias_rows", [BK, L, D], F32R, gnn_ctx)
            gamma = sb("gamma", [P, L, D], F32, gnn_ctx)
            beta = sb("beta", [P, L, D], F32, gnn_ctx)
            pack = [sb(f"pack{l}", [P, P], F32R, gnn_ctx) for l in range(L)]

            def per_layer_sb(name, shape, dt=F32):
                return [sb(f"{name}{l}", shape, dt, gnn_ctx) for l in range(L)]

            x_in = sb("x_in", [P, D], F32, gnn_ctx)
            x_res = sb("x_res", [P, D], F32, gnn_ctx)
            x1_out = sb("x1_out", [P, D], F32, gnn_ctx)
            relu_out = sb("relu_out", [P, D], F32, gnn_ctx)
            adj_in = per_layer_sb("adj_in", [P, P])
            masks = per_layer_sb("masks", [P, 3, P])
            h = per_layer_sb("h", [P, D])
            h_hi = per_layer_sb("h_hi", [P, D], F32R)
            h_lo = per_layer_sb("h_lo", [P, D], F32R)
            hT = per_layer_sb("hT", [P, D])
            hT_hi = per_layer_sb("hT_hi", [P, D], F32R)
            hT_lo = per_layer_sb("hT_lo", [P, D], F32R)
            expo = sb("expo", [P, P], F32, gnn_ctx)
            delta = sb("delta", [P, 3, P], F32, gnn_ctx)
            deltaT_hi = sb("deltaT_hi", [P, 2 * P], F32R, gnn_ctx)
            deltaT_lo = sb("deltaT_lo", [P, 2 * P], F32R, gnn_ctx)
            sumsT = per_layer_sb("sumsT", [BK, P], F32R)
            agg_hi = sb("agg_hi", [P, C, 2 * P], F32R, gnn_ctx)
            agg_lo = sb("agg_lo", [P, C, 2 * P], F32R, gnn_ctx)
            self_term = per_layer_sb("self_term", [P, D])
            ctx_sb = per_layer_sb("ctx_sb", [P, D])
            normed = per_layer_sb("normed", [P, D])
            ln1_bn = sb("ln1_bn", [P, 6], F32, gnn_ctx)
            ln1_mv = sb("ln1_mv", [P, 2], F32, gnn_ctx)
            ln1_t = sb("ln1_t", [P, 1], F32, gnn_ctx)
            ln1_scale = sb("ln1_scale", [P, 1], F32, gnn_ctx)
            ln1_shift = sb("ln1_shift", [P, 1], F32, gnn_ctx)
            row_max = per_layer_sb("row_max", [P, 1])
            neg_max = per_layer_sb("neg_max", [P, 1])
            exp_sum = per_layer_sb("exp_sum", [P, 1])
            sums = per_layer_sb("sums", [P, 3])
            sum_all = per_layer_sb("sum_all", [P, 1])
            denom = per_layer_sb("denom", [P, 1])
            inv_denom = per_layer_sb("inv_denom", [P, 1])
            bn = per_layer_sb("bn", [P, 6])
            mv = per_layer_sb("mv", [P, 2])
            var_n = per_layer_sb("var_n", [P, 1])
            var_e = per_layer_sb("var_e", [P, 1])
            rstd = per_layer_sb("rstd", [P, 1])
            out_scale = per_layer_sb("out_scale", [P, 1])

            x_loaded, xres_loaded, x1_stored = sem("x_loaded"), sem("xres_loaded"), sem("x1_stored")
            adj_loaded = per_layer("adj_loaded")
            ln1_bn_done, ln1_stats_done = sem("ln1_bn_done"), sem("ln1_stats_done")
            ln1_eps_added, ln1_rstd_done, ln1_scale_ready = sem("ln1_eps_added"), sem("ln1_rstd_done"), sem("ln1_scale_ready")
            h_ready, masks_ready = per_layer("h_ready"), per_layer("masks_ready")
            hT_done, hT_ready, hThi_ready, hTlo_ready = (per_layer(n) for n in (
                "hT_done", "hT_ready", "hThi_ready", "hTlo_ready"))
            hhi_ready, hlo_ready = per_layer("hhi_ready"), per_layer("hlo_ready")
            scores_done, max_done, negmax_ready, exp_done = (per_layer(n) for n in (
                "scores_done", "max_done", "negmax_ready", "exp_done"))
            sides_ready, delta_ready, sums_hi_done, sums_ready = (per_layer(n) for n in (
                "sides_ready", "delta_ready", "sums_hi_done", "sums_ready"))
            sum_done, denom_done, inv_done = (per_layer(n) for n in ("sum_done", "denom_done", "inv_done"))
            deltaT_done, deltaThi_ready, deltaTlo_ready, sumsT_done, sumsT_ready = (per_layer(n) for n in (
                "deltaT_done", "deltaThi_ready", "deltaTlo_ready", "sumsT_done", "sumsT_ready"))
            agg_done, agghi_ready, agglo_ready = (per_layer(n) for n in ("agg_done", "agghi_ready", "agglo_ready"))
            self_done, self_ready, ctx_done, ctx_ready = (per_layer(n) for n in (
                "self_done", "self_ready", "ctx_done", "ctx_ready"))
            bn_done, stats_done, scaled_once, eps_added, rstd_done, scale_ready = (per_layer(n) for n in (
                "bn_done", "stats_done", "scaled_once", "eps_added", "rstd_done", "scale_ready"))
            centred, tail_done = per_layer("centred"), per_layer("tail_done")
            relu_done, x1_ready = sem("relu_done"), sem("x1_ready")

            hT_bank, score_bank, deltaT_bank, self_bank, ctx_bank = bank[0], bank[1], bank[2], bank[3], bank[4]
            agg_bank = bank[5:8]
            route_parts = bank[3][:, 0:(C + 1) * E]

            def unit(s, l):
                return None if isinstance(s, int) and not 0 <= s < B else (s, l)

            def half_steps(i):
                return ((unit(i, 0), unit(i - 2, 1), unit(i - 1, 0), unit(i - 1, 1)),
                        (unit(i - 1, 1), unit(i, 0), unit(i - 2, 1), unit(i + 1, 0)))

            def before(s, l):
                if l == 0:
                    return unit(s - 2, 1) or unit(s - 1, 0)
                return unit(s + 1, 0) or unit(s - 1, 1)

            FIRST, LAST = 3, B - 2
            assert (LAST + 1 - FIRST) % 2 == 0

            def steps(eng, step):
                for i in range(1, FIRST):
                    step(i)
                with eng.Fori(0, (LAST + 1 - FIRST) // 2) as pair:
                    step(pair * 2 + FIRST)
                    step(pair * 2 + (FIRST + 1))
                for i in range(LAST + 1, B + 1):
                    step(i)

            CONST_LOADS, BIAS_LOADS = 7, 5

            with nc.Block() as block:
                @block.sync
                def _(sp):
                    def load_x(s):
                        if not isinstance(s, int) or s > 0:
                            sp.wait_ge(h_ready[0], s)
                        sp.dma_start(x_in[:], x[s, :, :]).then_inc(x_loaded, 16)

                    def load_adj(s, l):
                        if not isinstance(s, int) or s > 0:
                            sp.wait_ge(masks_ready[l], s)
                        sp.dma_start(adj_in[l][:], adj[s, :, :]).then_inc(adj_loaded[l], 16)

                    def load_residual(s):
                        if not isinstance(s, int) or s > 0:
                            sp.wait_ge(x1_ready, s)
                        sp.dma_start(x_res[:], x[s, :, :]).then_inc(xres_loaded, 16)

                    def step(i):
                        if isinstance(i, int) and i == B - 1:
                            sp.wait_ge(x1_stored, 16 * 2 * G)
                            sp.wait_ge(w_low_made, len(w_pieces))
                            for g in range(2):
                                sp.dma_start(x1[g][:], x1_groups[g, :, :, :]).then_inc(x1_loaded[g], 16)
                        if unit(i + 1, 0):
                            load_x(i + 1)
                            load_adj(i + 1, 0)
                        if unit(i, 0):
                            load_adj(i, 1)
                        if unit(i - 2, 1):
                            sp.wait_ge(x1_ready, i - 1)
                            sp.dma_start(x1_dram[i - 2, :, :], x1_out[:]).then_inc(x1_stored, 16)
                        if unit(i - 1, 1):
                            load_residual(i - 1)

                    load_x(0)
                    load_adj(0, 0)
                    for l in range(L):
                        for m, w in enumerate((Wl, Ws, Wr)):
                            sp.dma_start(stage[:, m, l, :, :],
                                         w[l, :, :].rearrange("(c p) d -> p c d", p=P)).then_inc(wt_in[l], 16)
                    sp.wait_ge(bias_zeroed, 2)
                    for row, b in enumerate((bl, bs, br)):
                        sp.dma_start(bias_in[row:row + 2 * SPLIT + 1:SPLIT, :, :],
                                     b.partition_broadcast(3)).then_inc(bias_in_loaded, 16)
                    for row in (0, SPLIT):
                        sp.dma_start(b2_in[row:row + E, :], b2).then_inc(bias_in_loaded, 16)
                    sp.dma_start(gamma[:], ln_w.partition_broadcast(P)).then_inc(const_in, 16)
                    sp.dma_start(beta[:], ln_b.partition_broadcast(P)).then_inc(const_in, 16)
                    sp.dma_start(b1_col[:], b1.rearrange("e r -> (e r)").rearrange("(q p) -> p q", p=P),
                                 allow_slow_non_contiguous=True).then_inc(const_in, 16)
                    step(0)
                    sp.wait_ge(wT_done, 3 * L * C)
                    for c in range(C):
                        sp.dma_start(w1_in[:, c, :].rearrange("p (e r) -> p e r", e=E),
                                     w1[:, c * P:(c + 1) * P, :].rearrange("e p r -> p e r")).then_inc(ffn_in, 16)
                    sp.dma_start(w2_in[:, :, :],
                                 w2.rearrange("e r d -> (e r) d").rearrange("(q p) d -> p q d", p=P)
                                 ).then_inc(ffn_in, 16)
                    steps(sp, step)
                    step(B + 1)
                    sp.wait_ge(x1_stored, 16 * B)

                @block.tensor
                def _(pe):
                    def transposes(s, l):
                        pe.wait_ge(h_ready[l], s + 1)
                        if before(s, l):
                            sb_, lb = before(s, l)
                            pe.wait_ge(hThi_ready[lb], sb_ + 1)
                        for c in range(C):
                            last = pe.transpose(hT_bank[:, c * P:(c + 1) * P], h[l][:, c * P:(c + 1) * P], ident[:])
                        last.then_inc(hT_done[l], 1)

                    def scores(s, l):
                        pe.wait_ge(hT_ready[l], s + 1)
                        if before(s, l):
                            sb_, lb = before(s, l)
                            pe.wait_ge(exp_done[lb], sb_ + 1)
                            pe.wait_ge(sumsT_ready[lb], sb_ + 1)
                        for c in range(C):
                            hc = hT[l][:, c * P:(c + 1) * P]
                            last = pe.matmul(score_bank[:, 0:P], hc, hc, start=(c == 0), stop=(c == C - 1))
                        last.then_inc(scores_done[l], 1)

                    def turn_delta(s, l):
                        pe.wait_ge(sides_ready[l], s + 1)
                        if before(s, l):
                            sb_, lb = before(s, l)
                            pe.wait_ge(deltaTlo_ready[lb], sb_ + 1)
                        pe.transpose(deltaT_bank[:, 0:P], delta[:, 0, :], ident[:])
                        pe.transpose(deltaT_bank[:, P:2 * P], delta[:, 2, :], ident[:]
                                     ).then_inc(deltaT_done[l], 1)

                    def turn_sums(s, l):
                        pe.wait_ge(sums_ready[l], s + 1)
                        pe.transpose(score_bank[:, 2 * P:3 * P].bitcast(F32R), pack[l][:], ident_r[:]
                                     ).then_inc(sumsT_done[l], 1)

                    def self_product(s, l, chunks):
                        if 0 in chunks:
                            pe.wait_ge(hThi_ready[l], s + 1)
                            pe.wait_ge(hTlo_ready[l], s + 1)
                            if before(s, l):
                                sb_, lb = before(s, l)
                                pe.wait_ge(self_ready[lb], sb_ + 1)
                        for c in chunks:
                            hi, lo = hT_hi[l][:, c * P:(c + 1) * P], hT_lo[l][:, c * P:(c + 1) * P]
                            w_hi, w_lo = wT_hi[:, l, 1, c, :], wT_lo[:, l, 1, c, :]
                            pe.matmul(self_bank[:, 0:D], hi, w_hi, start=(c == 0), stop=False)
                            pe.matmul(self_bank[:, 0:D], hi, w_lo, start=False, stop=False)
                            last = pe.matmul(self_bank[:, 0:D], lo, w_hi, start=False, stop=(c == C - 1))
                        if C - 1 in chunks:
                            last.then_inc(self_done[l], 1)

                    def neighbour_sums(s, l):
                        pe.wait_ge(hhi_ready[l], s + 1)
                        pe.wait_ge(hlo_ready[l], s + 1)
                        pe.wait_ge(deltaThi_ready[l], s + 1)
                        for c in range(C):
                            if before(s, l):
                                sb_, lb = before(s, l)
                                pe.wait_ge(agglo_ready[lb], C * sb_ + c + 1)
                            o = agg_bank[c][:, 0:2 * P]
                            hi, lo = h_hi[l][:, c * P:(c + 1) * P], h_lo[l][:, c * P:(c + 1) * P]
                            pe.matmul(o, hi, deltaT_hi[:], start=True, stop=False)
                            pe.matmul(o, lo, deltaT_hi[:], start=False, stop=False)
                            if c == 0:
                                pe.wait_ge(deltaTlo_ready[l], s + 1)
                            pe.matmul(o, hi, deltaT_lo[:], start=False, stop=True).then_inc(agg_done[l], 1)

                    def projection(s, l, chunks):
                        if 0 in chunks and before(s, l):
                            sb_, lb = before(s, l)
                            pe.wait_ge(ctx_ready[lb], sb_ + 1)
                        for c in chunks:
                            pe.wait_ge(agghi_ready[l], C * s + c + 1)
                            pe.wait_ge(agglo_ready[l], C * s + c + 1)
                            for side in range(2):
                                hi = agg_hi[:, c, side * P:(side + 1) * P]
                                lo = agg_lo[:, c, side * P:(side + 1) * P]
                                w_hi, w_lo = wT_hi[:, l, 2 * side, c, :], wT_lo[:, l, 2 * side, c, :]
                                pe.matmul(ctx_bank[:, 0:D], hi, w_hi, start=(c == 0 and side == 0), stop=False)
                                pe.matmul(ctx_bank[:, 0:D], hi, w_lo, start=False, stop=False)
                                pe.matmul(ctx_bank[:, 0:D], lo, w_hi, start=False, stop=False)

                    def biases(s, l):
                        pe.wait_ge(sumsT_ready[l], s + 1)
                        pe.matmul(ctx_bank[:, 0:D], sumsT[l][:], bias_rows[:, l, :],
                                  start=False, stop=True).then_inc(ctx_done[l], 1)

                    def make_router():
                        pe.wait_ge(const_in, 16 * CONST_LOADS)
                        pe.wait_ge(ctx_ready[0], 1)
                        pe.wait_ge(self_ready[0], 1)
                        for c in range(C):
                            last = pe.transpose(ctx_bank[0:R, c * P:(c + 1) * P], enc_in[:, c, :], ident[:])
                        last.then_inc(encT_done, 1)
                        pe.wait_ge(encT_made, 1)
                        pe.wait_ge(encb_made, 1)
                        for c in range(C):
                            pe.matmul(route_parts[:, c * E:(c + 1) * E], encT[:, c, :], sw_in[:], start=True, stop=True)
                        pe.matmul(route_parts[:, C * E:(C + 1) * E], encb_wide[:], sw_in[:],
                                  start=True, stop=True).then_inc(route_done, 1)

                    def turn_weights(l):
                        pe.wait_ge(wt_in[l], 16 * 3)
                        if l > 0:
                            pe.wait_ge(agglo_ready[0], C)
                        for m in range(3):
                            for dc in range(C):
                                n = (l * 3 + m) * C + dc
                                if n >= 3:
                                    pe.wait_ge(wT_lo_made, n - 2)
                                for oc in range(C):
                                    last = pe.transpose(agg_bank[n % 3][:, oc * P:(oc + 1) * P],
                                                        stage[:, m, l, oc, dc * P:(dc + 1) * P], ident[:])
                                last.then_inc(wT_done, 1)
                        pe.wait_ge(wT_lo_made, 3 * C * (l + 1))
                        pe.wait_ge(wT_hi_made, 3 * C * (l + 1))

                    def step(i, halves=(0, 1)):
                        for front, back, _, turned in [half_steps(i)[half] for half in halves]:
                            if back:
                                projection(*back, range(0, 1))
                            if front:
                                scores(*front)
                            if back:
                                projection(*back, range(1, C))
                            if front:
                                turn_delta(*front)
                            if back:
                                biases(*back)
                            if front:
                                self_product(*front, range(0, 1))
                                turn_sums(*front)
                                self_product(*front, range(1, C - 1))
                                neighbour_sums(*front)
                            if turned:
                                transposes(*turned)
                            if front:
                                self_product(*front, range(C - 1, C))

                    assert C == 3
                    turn_tokens, route, turn_logits, turn_one_hot, _ = ffn_tensor(pe)
                    pe.wait_ge(ident_made, 1)
                    transposes(0, 0)
                    turn_weights(0)
                    pe.wait_ge(ident_r_made, 1)
                    step(0, (0,))
                    pe.wait_ge(bias_made, 1)
                    step(0, (1,))
                    make_router()
                    turn_weights(1)
                    pe.wait_ge(route_made, 1)
                    steps(pe, step)
                    step(B + 1)
                    for c in range(C):
                        turn_tokens(0, c)
                    route(0, 0)
                    turn_logits(0)
                    turn_one_hot(0)

                @block.scalar
                def _(act):
                    def copy_hT(s, l):
                        act.wait_ge(hT_done[l], s + 1)
                        if not isinstance(s, int) or s > 0:
                            act.wait_ge(hTlo_ready[l], s)
                            act.wait_ge(scores_done[l], s)
                            act.wait_ge(self_done[l], s)
                        act.copy(hT[l][:], hT_bank[:, 0:D]).then_inc(hT_ready[l], 1)
                        act.copy(hT_hi[l][:], hT_bank[:, 0:D]).then_inc(hThi_ready[l], 1)

                    def self_weighting(s, l):
                        act.wait_ge(self_done[l], s + 1)
                        act.wait_ge(delta_ready[l], s + 1)
                        if not isinstance(s, int) or s > 0:
                            act.wait_ge(ctx_ready[l], s)
                        act.activation(self_term[l][:], self_bank[:, 0:D], ACT.Copy,
                                       scale=sums[l][:, 1:2]).then_inc(self_ready[l], 1)

                    def relu(s, l):
                        act.wait_ge(tail_done[l], s + 1)
                        if l == 0:
                            if not isinstance(s, int) or s > 0:
                                act.wait_ge(hT_done[1], s)
                                act.wait_ge(hhi_ready[1], s)
                                act.wait_ge(hlo_ready[1], s)
                            act.activation(h[1][:], normed[0][:], ACT.Relu).then_inc(h_ready[1], 1)
                        else:
                            if not isinstance(s, int) or s > 0:
                                act.wait_ge(x1_ready, s)
                            act.activation(relu_out[:], normed[1][:], ACT.Relu).then_inc(relu_done, 1)

                    def normalise_x(s):
                        act.wait_ge(ln1_scale_ready, s + 1)
                        if not isinstance(s, int) or s > 0:
                            act.wait_ge(hT_done[0], s)
                            act.wait_ge(hhi_ready[0], s)
                            act.wait_ge(hlo_ready[0], s)
                        act.activation(h[0][:], x_in[:], ACT.Identity, bias=ln1_shift[:, 0:1],
                                       scale=ln1_scale[:, 0:1]).then_inc(h_ready[0], 1)

                    def exponentials(s, l):
                        act.wait_ge(negmax_ready[l], s + 1)
                        if before(s, l):
                            sb_, lb = before(s, l)
                            act.wait_ge(delta_ready[lb], sb_ + 1)
                        act.activation(expo[:], score_bank[:, 0:P], ACT.Exp, bias=neg_max[l][:, 0:1],
                                       scale=float(D) ** -0.5, accum_out=exp_sum[l][:, 0:1]
                                       ).then_inc(exp_done[l], 1)

                    def copy_deltaT(s, l):
                        act.wait_ge(deltaT_done[l], s + 1)
                        if before(s, l):
                            sb_, lb = before(s, l)
                            act.wait_ge(agg_done[lb], C * (sb_ + 1))
                        act.copy(deltaT_hi[:], deltaT_bank[:, 0:2 * P]).then_inc(deltaThi_ready[l], 1)

                    def copy_sums(s, l):
                        act.wait_ge(sumsT_done[l], s + 1)
                        if not isinstance(s, int) or s > 0:
                            act.wait_ge(ctx_done[l], s)
                        act.copy(sumsT[l][:], score_bank[0:BK, 2 * P:3 * P]).then_inc(sumsT_ready[l], 1)

                    def copy_agg(s, l):
                        if before(s, l):
                            sb_, lb = before(s, l)
                            act.wait_ge(ctx_done[lb], sb_ + 1)
                        for c in range(C):
                            act.wait_ge(agg_done[l], C * s + c + 1)
                            act.copy(agg_hi[:, c, :], agg_bank[c][:, 0:2 * P]).then_inc(agghi_ready[l], 1)

                    def high_weights(l):
                        for m in range(3):
                            for dc in range(C):
                                n = (l * 3 + m) * C + dc
                                act.wait_ge(wT_done, n + 1)
                                act.copy(wT_hi[:, l, m, dc, :], agg_bank[n % 3][:, 0:D]).then_inc(wT_hi_made, 1)

                    def step(i, halves=(0, 1)):
                        for half in halves:
                            front, back, tail, _ = half_steps(i)[half]
                            if front and not (isinstance(i, int) and i == half == 0):
                                copy_hT(*front)
                            if back:
                                self_weighting(*back)
                            if front:
                                exponentials(*front)
                            if tail:
                                relu(*tail)
                            if half == 1 and unit(i + 1, 0):
                                normalise_x(i + 1)
                            if front:
                                copy_deltaT(*front)
                                copy_sums(*front)
                                copy_agg(*front)
                            for k in pieces(i, half):
                                act.wait_ge(ffn_in, 16 * (C + 1))
                                w_hi, _, w_raw = w_pieces[k]
                                act.copy(w_hi, w_raw).then_inc(w_high_made, 1)

                    act.dma_start(enc_in[:], enc_w.rearrange("(c p) r -> p c r", p=P)).then_inc(const_in, 16)
                    act.dma_start(sw_in[:], sw_w).then_inc(const_in, 16)
                    act.dma_start(encb_col[:], enc_b.rearrange("(r a) -> r a", a=1)).then_inc(const_in, 16)
                    act.dma_start(swb_all[:], sw_b.partition_broadcast(P)).then_inc(const_in, 16)

                    normalise, copy_tokensT, copy_logitsT, copy_one_hotT, _ = ffn_scalar(act)
                    normalise_x(0)
                    copy_hT(0, 0)
                    high_weights(0)
                    step(0)
                    act.wait_ge(encT_done, 1)
                    act.copy(encT[:], ctx_bank[0:R, 0:C * P].rearrange("r (c p) -> r c p", c=C)
                             ).then_inc(encT_made, 1)
                    high_weights(1)
                    steps(act, step)
                    normalise(0, 0)
                    step(B + 1, (0,))
                    for c in range(C):
                        copy_tokensT(0, 0, c)
                    step(B + 1, (1,))
                    copy_logitsT(0)
                    copy_one_hotT(0, 0)

                @block.vector
                def _(dve):
                    def x_stats(s):
                        dve.wait_ge(x_loaded, 16 * (s + 1))
                        dve.bn_stats(ln1_bn[:], x_in[:]).then_inc(ln1_bn_done, 1)

                    def x_moments(s):
                        dve.wait_ge(ln1_bn_done, s + 1)
                        if not isinstance(s, int) or s > 0:
                            dve.wait_ge(ln1_scale_ready, s)
                        dve.nop(nofuse=True)
                        dve.bn_aggr(ln1_mv[:], ln1_bn[:]).then_inc(ln1_stats_done, 1)

                    def split_h(s, l):
                        dve.wait_ge(h_ready[l], s + 1)
                        if not isinstance(s, int) or s > 0:
                            dve.wait_ge(agg_done[l], C * s)
                            dve.wait_ge(hlo_ready[l], s)
                        dve.tensor_copy(h_hi[l][:], h[l][:]).then_inc(hhi_ready[l], 1)

                    def row_maximum(s, l):
                        dve.wait_ge(scores_done[l], s + 1)
                        dve.tensor_reduce(row_max[l][:], score_bank[:, 0:P], AX_X, ALU.max).then_inc(max_done[l], 1)
                        dve.wait_ge(max_done[l], s + 1)
                        dve.tensor_scalar(neg_max[l][:], row_max[l][:], -float(D) ** -0.5, None,
                                          ALU.mult).then_inc(negmax_ready[l], 1)

                    def masked_sums(s, l):
                        dve.wait_ge(exp_done[l], s + 1)
                        dve.wait_ge(masks_ready[l], s + 1)
                        if before(s, l):
                            sb_, lb = before(s, l)
                            dve.wait_ge(deltaT_done[lb], sb_ + 1)
                        for side, ready in ((0, None), (2, sides_ready), (1, delta_ready)):
                            ttr = dve.tensor_tensor_reduce(delta[:, side, :], expo[:], masks[l][:, side, :],
                                                           1.0, 0.0, ALU.mult, ALU.add, sums[l][:, side:side + 1])
                            if ready:
                                ttr.then_inc(ready[l], 1)

                    def pack_sums(s, l):
                        dve.wait_ge(delta_ready[l], s + 1)
                        if not isinstance(s, int) or s > 0:
                            dve.wait_ge(sumsT_done[l], s)
                        dve.tensor_copy(pack[l][:, 0:2 * SPLIT].rearrange("p (a b) -> p a b", a=2)[:, :, 0:3],
                                        sums[l][:].unsqueeze(1).broadcast_to([P, 2, 3])
                                        ).then_inc(sums_hi_done[l], 1)
                        dve.scalar_tensor_tensor(sum_all[l][:], sums[l][:, 0:1], sums[l][:, 1:2], sums[l][:, 2:3],
                                                 ALU.add, ALU.add).then_inc(sum_done[l], 1)
                        dve.wait_ge(sums_hi_done[l], s + 1)
                        dve.tensor_tensor(pack[l][:, 2 * SPLIT:BK], sums[l][:], pack[l][:, 0:3].bitcast(F32),
                                          ALU.subtract).then_inc(sums_ready[l], 1)

                    def denominator(s, l):
                        dve.wait_ge(sum_done[l], s + 1)
                        dve.scalar_tensor_tensor(denom[l][:], exp_sum[l][:], DENOM_EPS, sum_all[l][:],
                                                 ALU.mult, ALU.add).then_inc(denom_done[l], 1)

                    def inverse(s, l):
                        dve.wait_ge(denom_done[l], s + 1)
                        if not isinstance(s, int) or s > 0:
                            dve.wait_ge(scale_ready[l], s)
                        dve.reciprocal(inv_denom[l][:], denom[l][:]).then_inc(inv_done[l], 1)

                    def add_self(s, l):
                        dve.wait_ge(ctx_done[l], s + 1)
                        dve.wait_ge(self_ready[l], s + 1)
                        dve.tensor_tensor(ctx_sb[l][:], ctx_bank[:, 0:D], self_term[l][:], ALU.add
                                          ).then_inc(ctx_ready[l], 1)

                    def ctx_stats(s, l):
                        dve.wait_ge(ctx_ready[l], s + 1)
                        dve.bn_stats(bn[l][:], ctx_sb[l][:]).then_inc(bn_done[l], 1)

                    def ctx_moments(s, l):
                        dve.wait_ge(bn_done[l], s + 1)
                        dve.nop(nofuse=True)
                        dve.bn_aggr(mv[l][:], bn[l][:]).then_inc(stats_done[l], 1)

                    def centre(s, l):
                        dve.wait_ge(stats_done[l], s + 1)
                        if not isinstance(s, int) or s > 0:
                            dve.wait_ge(h_ready[1] if l == 0 else relu_done, s)
                        dve.scalar_tensor_tensor(normed[l][:], ctx_sb[l][:], mv[l][:, 0:1], gamma[:, l, :],
                                                 ALU.subtract, ALU.mult).then_inc(centred[l], 1)

                    def scale_shift(s, l):
                        dve.wait_ge(scale_ready[l], s + 1)
                        dve.wait_ge(centred[l], s + 1)
                        dve.scalar_tensor_tensor(normed[l][:], normed[l][:], out_scale[l][:, 0:1], beta[:, l, :],
                                                 ALU.mult, ALU.add).then_inc(tail_done[l], 1)

                    def deltaT_low(s, l):
                        dve.wait_ge(deltaThi_ready[l], s + 1)
                        dve.tensor_tensor(deltaT_lo[:], deltaT_bank[:, 0:2 * P], deltaT_hi[:].bitcast(F32),
                                          ALU.subtract).then_inc(deltaTlo_ready[l], 1)

                    def agg_low(s, l, c):
                        dve.wait_ge(agghi_ready[l], C * s + c + 1)
                        dve.tensor_tensor(agg_lo[:, c, :], agg_bank[c][:, 0:2 * P],
                                          agg_hi[:, c, :].bitcast(F32), ALU.subtract
                                          ).then_inc(agglo_ready[l], 1)

                    def low_weights(l):
                        for m in range(3):
                            for dc in range(C):
                                n = (l * 3 + m) * C + dc
                                dve.wait_ge(wT_hi_made, n + 1)
                                dve.tensor_tensor(wT_lo[:, l, m, dc, :], agg_bank[n % 3][:, 0:D],
                                                  wT_hi[:, l, m, dc, :].bitcast(F32),
                                                  ALU.subtract).then_inc(wT_lo_made, 1)

                    def constants():
                        dve.memset(switch_off[:].bitcast(F32), 0.0)
                        dve.memset(route_w[:].bitcast(F32), 0.0)
                        for l in range(L):
                            dve.memset(pack[l][:].bitcast(F32), 0.0)
                        dve.memset(one_hot[:].bitcast(F32), 0.0)
                        dve.memset(ones[:], 1.0).then_inc(filled, 1)
                        dve.wait_ge(ident_made, 1)
                        dve.tensor_copy(ident_r[:], ident[:]).then_inc(ident_r_made, 1)
                        dve.wait_ge(filled, 1)
                        dve.tensor_scalar(switch_off[0:E, :, :].rearrange("k q (h r) -> k (q h) r", h=P // R),
                                          ident[0:E, 0:E].unsqueeze(2).broadcast_to([E, E, R]),
                                          SWITCHED_OFF, -SWITCHED_OFF, ALU.mult, ALU.add)

                    def biases():
                        dve.wait_ge(bias_in_loaded, 16 * BIAS_LOADS)
                        dve.tensor_copy(bias_rows[:], bias_in[:]).then_inc(bias_high_made, 1)
                        dve.tensor_copy(b2_rows[:], b2_in[:]).then_inc(b2_high_made, 1)
                        dve.wait_ge(bias_high_made, 1)
                        dve.tensor_tensor(bias_rows[SPLIT:SPLIT + 3, :, :], bias_in[SPLIT:SPLIT + 3, :, :],
                                          bias_rows[SPLIT:SPLIT + 3, :, :].bitcast(F32), ALU.subtract
                                          ).then_inc(bias_made, 1)
                        dve.wait_ge(b2_high_made, 1)
                        dve.tensor_tensor(b2_rows[SPLIT:SPLIT + E, :], b2_in[SPLIT:SPLIT + E, :],
                                          b2_rows[SPLIT:SPLIT + E, :].bitcast(F32), ALU.subtract)

                    def router():
                        dve.wait_ge(route_done, 1)
                        by_chunk = route_parts[:, 0:C * E].rearrange("p (c e) -> p c e", c=C)
                        dve.tensor_copy(route_w[:, :, 0:E], by_chunk).then_inc(route_hi_made, 1)
                        dve.wait_ge(route_hi_made, 1)
                        dve.tensor_tensor(route_w[:, :, SPLIT:SPLIT + E], by_chunk,
                                          route_w[:, :, 0:E].bitcast(F32), ALU.subtract)
                        dve.tensor_tensor(route_b[:], route_parts[:, C * E:(C + 1) * E], swb_all[:], ALU.add
                                          ).then_inc(route_made, 1)

                    def step(i, halves=(0, 1)):
                        for half in halves:
                            front, back, tail, _ = half_steps(i)[half]
                            if front:
                                split_h(*front)
                                row_maximum(*front)
                            if tail:
                                scale_shift(*tail)
                            if front:
                                masked_sums(*front)
                                pack_sums(*front)
                                denominator(*front)
                                inverse(*front)
                                deltaT_low(*front)
                            if back:
                                add_self(*back)
                                ctx_stats(*back)
                            if half == 0 and unit(i + 1, 0):
                                x_stats(i + 1)
                            if half == 1 and isinstance(i, int) and i == B:
                                stats(0, 0)
                            if front:
                                agg_low(*front, 0)
                            if half == 0 and unit(i + 1, 0):
                                x_moments(i + 1)
                            if back:
                                ctx_moments(*back)
                            if front:
                                agg_low(*front, 1)
                                agg_low(*front, 2)
                            if back:
                                centre(*back)
                            for k in pieces(i, half):
                                dve.wait_ge(w_high_made, k + 1)
                                w_hi, w_lo, w_raw = w_pieces[k]
                                dve.tensor_tensor(w_lo, w_raw, w_hi.bitcast(F32), ALU.subtract
                                                  ).then_inc(w_low_made, 1)

                    assert C == 3
                    stats, normalise, tokensT_low, route_first, route_second, _ = ffn_vector(dve)
                    constants()
                    x_stats(0)
                    x_moments(0)
                    low_weights(0)
                    step(0, (0,))
                    biases()
                    dve.wait_ge(const_in, 16 * CONST_LOADS)
                    dve.tensor_scalar(encb_wide[:], ones[:], encb_col[:, 0:1], None, ALU.mult
                                      ).then_inc(encb_made, 1)
                    step(0, (1,))
                    low_weights(1)
                    router()
                    steps(dve, step)
                    normalise(0, 0)
                    step(B + 1, (0,))
                    for c in range(C):
                        tokensT_low(0, 0, c)
                    step(B + 1, (1,))
                    route_first(0)
                    route_second(0)

                @block.gpsimd
                def _(pool):
                    def split_hT(s, l):
                        pool.wait_ge(hThi_ready[l], s + 1)
                        pool.tensor_tensor(hT_lo[l][:], hT[l][:], hT_hi[l][:].bitcast(F32), ALU.subtract
                                           ).then_inc(hTlo_ready[l], 1)

                    def split_h(s, l):
                        pool.wait_ge(hhi_ready[l], s + 1)
                        pool.tensor_tensor(h_lo[l][:], h[l][:], h_hi[l][:].bitcast(F32), ALU.subtract
                                           ).then_inc(hlo_ready[l], 1)

                    def residual(s):
                        pool.wait_ge(relu_done, s + 1)
                        pool.wait_ge(xres_loaded, 16 * (s + 1))
                        if not isinstance(s, int) or s > 0:
                            pool.wait_ge(x1_stored, 16 * s)
                        pool.tensor_tensor(x1_out[:], relu_out[:], x_res[:], ALU.add).then_inc(x1_ready, 1)

                    def make_masks(s, l):
                        pool.wait_ge(adj_loaded[l], 16 * (s + 1))
                        if not isinstance(s, int) or s > 0:
                            pool.wait_ge(delta_ready[l], s)
                        pool.nop(nofuse=True)
                        pool.affine_select(out=masks[l][:, 0, :], in_=adj_in[l][:], compare_op=ALU.is_gt, fill=0.0,
                                           base=0, pattern=[[1, P]], channel_multiplier=-1)
                        pool.affine_select(out=masks[l][:, 1, :], in_=adj_in[l][:], compare_op=ALU.is_equal,
                                           fill=0.0, base=0, pattern=[[1, P]], channel_multiplier=-1)
                        pool.affine_select(out=masks[l][:, 2, :], in_=adj_in[l][:], compare_op=ALU.is_gt, fill=0.0,
                                           base=0, pattern=[[-1, P]], channel_multiplier=1
                                           ).then_inc(masks_ready[l], 1)

                    def layer_scale(s, l):
                        pool.wait_ge(stats_done[l], s + 1)
                        pool.wait_ge(inv_done[l], s + 1)
                        if not isinstance(s, int) or s > 0:
                            pool.wait_ge(tail_done[l], s)
                        pool.nop(nofuse=True)
                        pool.tensor_scalar(var_n[l][:], mv[l][:, 1:2], inv_denom[l][:, 0:1], inv_denom[l][:, 0:1],
                                           ALU.mult, ALU.mult).then_inc(scaled_once[l], 1)
                        pool.wait_ge(scaled_once[l], s + 1)
                        pool.nop(nofuse=True)
                        pool.tensor_scalar(var_e[l][:], var_n[l][:], LN_LAYER_EPS, None, ALU.add
                                           ).then_inc(eps_added[l], 1)
                        pool.wait_ge(eps_added[l], s + 1)
                        pool.tensor_tensor(rstd[l][:], var_e[l][:], minus_half[:, 0:1], ALU.pow
                                           ).then_inc(rstd_done[l], 1)
                        pool.wait_ge(rstd_done[l], s + 1)
                        pool.tensor_tensor(out_scale[l][:], rstd[l][:], inv_denom[l][:], ALU.mult
                                           ).then_inc(scale_ready[l], 1)

                    def x_scale(s):
                        pool.wait_ge(ln1_stats_done, s + 1)
                        if not isinstance(s, int) or s > 0:
                            pool.wait_ge(h_ready[0], s)
                        pool.nop(nofuse=True)
                        pool.tensor_scalar(ln1_t[:], ln1_mv[:, 1:2], LN_INPUT_EPS, None, ALU.add
                                           ).then_inc(ln1_eps_added, 1)
                        pool.wait_ge(ln1_eps_added, s + 1)
                        pool.tensor_tensor(ln1_scale[:], ln1_t[:], minus_half[:, 0:1], ALU.pow
                                           ).then_inc(ln1_rstd_done, 1)
                        pool.wait_ge(ln1_rstd_done, s + 1)
                        pool.nop(nofuse=True)
                        pool.tensor_scalar(ln1_shift[:], ln1_mv[:, 0:1], ln1_scale[:, 0:1], -1.0,
                                           ALU.mult, ALU.mult).then_inc(ln1_scale_ready, 1)

                    def step(i, halves=(0, 1)):
                        for half in halves:
                            front, back, tail, turned = half_steps(i)[half]
                            if front:
                                split_hT(*front)
                                split_h(*front)
                            if tail and tail[1] == 1:
                                residual(tail[0])
                            if turned:
                                make_masks(*turned)
                            if back:
                                layer_scale(*back)
                            if half == 0 and unit(i + 1, 0):
                                x_scale(i + 1)

                    token_scale, exponentials, _ = ffn_gpsimd(pool)
                    pool.memset(bias_in[:], 0.0).then_inc(bias_zeroed, 1)
                    pool.memset(b2_in[:], 0.0).then_inc(bias_zeroed, 1)
                    pool.memset(minus_half[:], -0.5)
                    pool.memset(ident[:], 0.0).then_inc(zeroed, 1)
                    pool.wait_ge(zeroed, 1)
                    pool.nop(nofuse=True)
                    pool.affine_select(out=ident[:], in_=ident[:], compare_op=ALU.not_equal, fill=1.0,
                                       base=0, pattern=[[-1, P]], channel_multiplier=1).then_inc(ident_made, 1)
                    pool.memset(euler[:], float(np.e))
                    for e in range(E):
                        last = pool.memset(rank[:, :, e:e + 1], float(E - e))
                    last.then_inc(consts_made, 1)
                    x_scale(0)
                    make_masks(0, 0)
                    step(0)
                    steps(pool, step)
                    token_scale(0)
                    step(B + 1)
                    exponentials(0)

        ffn_ctx = ExitStack()
        with ffn_ctx:
            x1 += [sb(f"x1_{r}", [P, G, D], F32, ffn_ctx) for r in range(2, RING)]
            oneT.append(sb("oneT1", [ROUTE, TOK], F32R, ffn_ctx))
            n2T_hi.append(sb("n2T_hi1", [P, C, TOK], F32R, ffn_ctx))
            n2T_lo.append(sb("n2T_lo1", [P, C, TOK], F32R, ffn_ctx))
            out_sb = [sb(f"out_sb{k}", [P, G, D], F32, ffn_ctx) for k in range(2)]
            gelu_out = sb("gelu_out", [P, Q, TOK], F32, ffn_ctx)
            gelu_hi = sb("gelu_hi", [P, Q, TOK], F32R, ffn_ctx)
            gelu_lo = sb("gelu_lo", [P, Q, TOK], F32R, ffn_ctx)
            def groups(eng, group):
                for g in range(RING):
                    group(g, g)
                with eng.Fori(1, NG // RING - 1) as i:
                    for r in range(RING):
                        group(i * RING + r, r)
                for g in range(NG - RING, NG):
                    group(g, g % RING)

            with nc.Block() as block:
                @block.sync
                def _(sp):
                    def load(g, r):
                        if not isinstance(g, int) or g >= RING:
                            sp.wait_ge(y_ready, G * (g - RING + 1))
                        sp.dma_start(x1[r][:], x1_groups[g, :, :, :]).then_inc(x1_loaded[r], 16)

                    def group(g, r):
                        if there(g + 2):
                            load(g + 2, (r + 2) % RING)
                        if isinstance(g, int) and g == NG - 1:
                            for t in range(G):
                                sp.wait_ge(y_ready, G * g + t + 1)
                                sp.dma_start(out_groups[g, :, t, :], out_sb[r % 2][:, t, :]
                                             ).then_inc(out_stored[r % 2], 16)
                            return
                        sp.wait_ge(y_ready, G * (g + 1))
                        sp.dma_start(out_groups[g, :, :, :], out_sb[r % 2][:]).then_inc(out_stored[r % 2], 16)

                    groups(sp, group)
                    sp.wait_ge(out_stored[0], 8 * NG)
                    sp.wait_ge(out_stored[1], 8 * NG + 16 * (G - 1))

                @block.tensor
                def _(pe):
                    *_, group = ffn_tensor(pe)
                    groups(pe, group)

                @block.scalar
                def _(act):
                    *_, group = ffn_scalar(act)
                    groups(act, group)

                @block.vector
                def _(dve):
                    stats, *_, group = ffn_vector(dve)
                    stats(1, 1)
                    groups(dve, group)

                @block.gpsimd
                def _(pool):
                    *_, group = ffn_gpsimd(pool)
                    groups(pool, group)


_INS = ["x", "adj", "L0_gnn_Wl", "L0_gnn_bl", "L0_gnn_Ws", "L0_gnn_bs", "L0_gnn_Wr", "L0_gnn_br",
        "L0_gnn_ln_w", "L0_gnn_ln_b", "L0_ffn_enc_w", "L0_ffn_enc_b", "L0_ffn_sw_w", "L0_ffn_sw_b",
        "L0_ffn_w1", "L0_ffn_b1", "L0_ffn_w2", "L0_ffn_b2"]
_OUTS = [((128, 128, 384), "float32")]


def kernel(**inputs):
    import numpy as _np
    import concourse.bacc as _bacc
    from concourse import mybir as _mybir
    from concourse.bass_utils import run_bass_kernel_spmd as _run

    nc = _bacc.Bacc("TRN2", target_bir_lowering=False, num_devices=1)
    arrays, args = {}, []
    for name in _INS:
        a = _np.ascontiguousarray(inputs[name])
        arrays[f"in_{name}_dram"] = a
        args.append(nc.dram_tensor(f"in_{name}_dram", a.shape, _mybir.dt.from_np(a.dtype), kind="ExternalInput").ap())
    for i, (shape, dtype) in enumerate(_OUTS):
        dt = _mybir.dt.from_np(_np.dtype(dtype))
        args.append(nc.dram_tensor(f"out_{i}_dram", shape, dt, kind="ExternalOutput").ap())
    build(nc, *args)
    r = _run(nc, [arrays], core_ids=[0])
    got = tuple(r.results[0][f"out_{i}_dram"] for i in range(len(_OUTS)))
    return got[0]
```
